# Optimizing a Trainium2 kernel written in Bass

```python
import numpy as np
import jax
import jax.numpy as jnp

def _softmax(x, axis=-1):
    return jax.nn.softmax(x, axis=axis)

def _gelu(x):
    return jax.nn.gelu(x, approximate=True)

def _silu(x):
    return jax.nn.silu(x)

def _sigmoid(x):
    return jax.nn.sigmoid(x)

def _layernorm(x, axis=-1, eps=1e-05):
    m = jnp.mean(x, axis=axis, keepdims=True)
    v = jnp.var(x, axis=axis, keepdims=True)
    return (x - m) / jnp.sqrt(v + eps)

def _scatter_add(tgt, idx, src, axis=0):
    return tgt.at[idx].add(src)

def _segment_sum(src, seg, n):
    return jax.ops.segment_sum(src, seg, n)
kernel_name = 'mk_prb_d4_jaxref_r8_2ae51d'

def setup_inputs(seed: int=0):
    np.random.seed(seed)
    _w = jnp.asarray

    def _L0_attn_setup():
        import jax, jax.numpy as jnp
        import numpy as np
        BSZ, T, DM, N = (8, 512, 128, 64)
        LN_EPS = 1e-05
        key = jax.random.key(seed)
        ks = jax.random.split(key, 7)
        return {'x': jax.random.normal(ks[0], (BSZ, T, DM), jnp.float32), 'log_A': jax.random.normal(ks[1], (DM, N), jnp.float32) * 0.01 - 4.0, 'B_param': jax.random.normal(ks[2], (DM, N), jnp.float32) * 0.01, 'C_param': jax.random.normal(ks[3], (DM, N), jnp.float32) * 0.01, 'D_param': jnp.ones((DM,), jnp.float32), 'log_dt': jax.random.normal(ks[4], (DM,), jnp.float32) * 0.01 - 4.0, 'ln_gamma': jnp.ones((DM,), jnp.float32), 'ln_beta': jnp.zeros((DM,), jnp.float32), 'W_out': jax.random.normal(ks[5], (DM, DM), jnp.float32) / np.sqrt(DM).astype(np.float32), 'b_out': jnp.zeros((DM,), jnp.float32)}
    _L0_attn_in = _L0_attn_setup()

    def _L0_ffn_setup():
        import jax, jax.numpy as jnp
        import numpy as np
        EPS = 1e-05
        LN_EPS = 1e-05
        NUM_EXPERTS = 8
        TOP_K = 2
        HIDDEN = 128
        INTER = 256

        def _swiglu(x, wg, wu, wd):
            return jax.nn.silu(x @ wg) * (x @ wu) @ wd
        key = jax.random.key(seed)
        ks = jax.random.split(key, 10)
        B, S, H, I, E = (8, 512, HIDDEN, INTER, NUM_EXPERTS)
        std_h = 1.0 / np.sqrt(H)
        std_i = 1.0 / np.sqrt(I)
        return {'x': jax.random.normal(ks[0], (B, S, H), dtype=jnp.float32), 'ln_scale': jnp.ones((H,), dtype=jnp.float32), 'ln_bias': jnp.zeros((H,), dtype=jnp.float32), 'gate_w': jax.random.normal(ks[1], (E, H), dtype=jnp.float32) * 0.01, 'Wg': jax.random.normal(ks[2], (E, H, I), dtype=jnp.float32) * std_h, 'Wu': jax.random.normal(ks[3], (E, H, I), dtype=jnp.float32) * std_h, 'Wd': jax.random.normal(ks[4], (E, I, H), dtype=jnp.float32) * std_i, 'sWg': jax.random.normal(ks[5], (H, I), dtype=jnp.float32) * std_h, 'sWu': jax.random.normal(ks[6], (H, I), dtype=jnp.float32) * std_h, 'sWd': jax.random.normal(ks[7], (I, H), dtype=jnp.float32) * std_i}
    _L0_ffn_in = _L0_ffn_setup()

    def _L1_attn_setup():
        import jax, jax.numpy as jnp
        import numpy as np
        B, S, D_IN, D_OUT, H = (4, 256, 128, 128, 16)
        HD = D_OUT // H
        key = jax.random.key(seed)
        ks = jax.random.split(key, 6)
        s = 1.0 / np.sqrt(D_IN)
        return {'x': jax.random.normal(ks[0], (B, S, D_IN), dtype=jnp.float32), 'Wq': jax.random.uniform(ks[1], (D_IN, D_OUT), jnp.float32, -s, s), 'Wk': jax.random.uniform(ks[2], (D_IN, D_OUT), jnp.float32, -s, s), 'Wv': jax.random.uniform(ks[3], (D_IN, D_OUT), jnp.float32, -s, s), 'Wo': jax.random.uniform(ks[4], (D_OUT, D_OUT), jnp.float32, -s, s), 'bo': jax.random.uniform(ks[5], (D_OUT,), jnp.float32, -s, s)}
    _L1_attn_in = _L1_attn_setup()

    def _L1_ffn_setup():
        import jax, jax.numpy as jnp
        import numpy as np
        DIM = 128
        HIDDEN = 384
        SCALE = 1.0 / 127.0

        def _dequant(w_int, dtype):
            return w_int.astype(dtype) * jnp.asarray(SCALE, dtype)
        key = jax.random.key(seed)
        k_x, k_g, k_u, k_d = jax.random.split(key, 4)
        x = jax.random.normal(k_x, (4, 256, DIM), dtype=jnp.float32)
        w_gate = jax.random.randint(k_g, (HIDDEN, DIM), -127, 128, dtype=jnp.int32)
        w_up = jax.random.randint(k_u, (HIDDEN, DIM), -127, 128, dtype=jnp.int32)
        w_down = jax.random.randint(k_d, (DIM, HIDDEN), -127, 128, dtype=jnp.int32)
        return {'x': x, 'w_gate': w_gate, 'w_up': w_up, 'w_down': w_down}
    _L1_ffn_in = _L1_ffn_setup()

    def _L2_attn_setup():
        import jax, jax.numpy as jnp
        import numpy as np
        N_EMBD = 128
        N_HEAD = 16
        HEAD_SIZE = N_EMBD // N_HEAD
        WINDOW = 3

        def _shift(a, j):
            if j == 0:
                return a
            return jnp.pad(a, ((0, 0), (0, 0), (j, 0), (0, 0)))[:, :, :-j, :]
        key = jax.random.key(seed)
        ks = jax.random.split(key, 9)
        C = N_EMBD
        s = 1.0 / np.sqrt(C)
        x = jax.random.normal(ks[0], (8, 512, C), dtype=jnp.float32)
        Wq = jax.random.uniform(ks[1], (C, C), jnp.float32, -s, s)
        Wk = jax.random.uniform(ks[2], (C, C), jnp.float32, -s, s)
        Wv = jax.random.uniform(ks[3], (C, C), jnp.float32, -s, s)
        Wo = jax.random.uniform(ks[4], (C, C), jnp.float32, -s, s)
        bq = jax.random.uniform(ks[5], (C,), jnp.float32, -s, s)
        bk = jax.random.uniform(ks[6], (C,), jnp.float32, -s, s)
        bv = jax.random.uniform(ks[7], (C,), jnp.float32, -s, s)
        bo = jax.random.uniform(ks[8], (C,), jnp.float32, -s, s)
        return {'x': x, 'Wq': Wq, 'bq': bq, 'Wk': Wk, 'bk': bk, 'Wv': Wv, 'bv': bv, 'Wo': Wo, 'bo': bo}
    _L2_attn_in = _L2_attn_setup()

    def _L2_ffn_setup():
        import jax, jax.numpy as jnp
        import numpy as np
        D_IN, D_HID = (128, 512)

        def _ternary(key, shape):
            return jax.random.randint(key, shape, -1, 2).astype(jnp.float32)

        def _tlin(x, w, s):
            return jnp.einsum('bsi,oi->bso', x, w) * s
        key = jax.random.key(seed)
        ks = jax.random.split(key, 12)
        inv = lambda fan: 1.0 / np.sqrt(fan).astype(np.float32)
        return {'x': jax.random.normal(ks[0], (4, 256, D_IN), dtype=jnp.float32), 'w1_w': _ternary(ks[1], (D_HID, D_IN)), 'w1_s': jax.random.uniform(ks[2], (D_HID,), dtype=jnp.float32) * inv(D_IN), 'w2_w': _ternary(ks[3], (D_HID, D_IN)), 'w2_s': jax.random.uniform(ks[4], (D_HID,), dtype=jnp.float32) * inv(D_IN), 'h1_w': _ternary(ks[5], (D_HID, D_HID)), 'h1_s': jax.random.uniform(ks[6], (D_HID,), dtype=jnp.float32) * inv(D_HID), 'h2_w': _ternary(ks[7], (D_HID, D_HID)), 'h2_s': jax.random.uniform(ks[8], (D_HID,), dtype=jnp.float32) * inv(D_HID), 'w3_w': _ternary(ks[9], (D_IN, D_HID)), 'w3_s': jax.random.uniform(ks[10], (D_IN,), dtype=jnp.float32) * inv(D_HID)}
    _L2_ffn_in = _L2_ffn_setup()

    def _L3_attn_setup():
        import jax, jax.numpy as jnp
        import numpy as np
        from math import sqrt
        EMBED_DIM = 128
        NUM_HEADS = 16
        HEAD_DIM = EMBED_DIM // NUM_HEADS
        CAUSAL = True
        key = jax.random.key(seed)
        ks = jax.random.split(key, 5)
        B, S, E = (2, 256, EMBED_DIM)
        x = jax.random.normal(ks[0], (B, S, E), dtype=jnp.float32)
        scale = 1.0 / sqrt(E)
        Wq = jax.random.normal(ks[1], (E, E), dtype=jnp.float32) * scale
        Wk = jax.random.normal(ks[2], (E, E), dtype=jnp.float32) * scale
        Wv = jax.random.normal(ks[3], (E, E), dtype=jnp.float32) * scale
        Wo = jax.random.normal(ks[4], (E, E), dtype=jnp.float32) * scale
        return {'x': x, 'Wq': Wq, 'Wk': Wk, 'Wv': Wv, 'Wo': Wo}
    _L3_attn_in = _L3_attn_setup()

    def _L3_ffn_setup():
        import jax, jax.numpy as jnp
        import numpy as np
        B, S, DIM = (4, 512, 128)
        BASE_COUPLING = 0.1
        NUM_CYCLES = 3

        def _gelu(x):
            return jax.nn.gelu(x, approximate=False)

        def _coupling_net(h, w1, b1, w2, b2, w3, b3, w4, b4):
            h = _gelu(h @ w1 + b1)
            h = _gelu(h @ w2 + b2)
            h = _gelu(h @ w3 + b3)
            return jax.nn.sigmoid(h @ w4 + b4)

        def _global_net(h, w1, b1, w2, b2, w3, b3):
            h = _gelu(h @ w1 + b1)
            h = _gelu(h @ w2 + b2)
            return jax.nn.sigmoid(h @ w3 + b3)

        def _twist(x):
            o_r, o_i, p_r, p_i = jnp.split(x, 4, axis=-1)
            return jnp.concatenate([p_r, -p_i, -o_r, o_i], axis=-1)
        key = jax.random.key(seed)
        ks = jax.random.split(key, 9)
        d = DIM

        def w(k, fan_in, fan_out):
            return jax.random.normal(k, (fan_in, fan_out), dtype=jnp.float32) / np.sqrt(fan_in).astype(np.float32)
        inp = {'x': jax.random.normal(ks[0], (B, S, d), dtype=jnp.float32)}
        cn_dims = [(d, d), (d, d // 2), (d // 2, d // 4), (d // 4, 1)]
        for i, (a, b) in enumerate(cn_dims):
            inp[f'cn_w{i + 1}'] = w(ks[1 + i], a, b)
            inp[f'cn_b{i + 1}'] = jnp.zeros((b,), dtype=jnp.float32)
        gc_dims = [(d, d // 2), (d // 2, d // 4), (d // 4, 1)]
        for i, (a, b) in enumerate(gc_dims):
            inp[f'gc_w{i + 1}'] = w(ks[5 + i], a, b)
            inp[f'gc_b{i + 1}'] = jnp.zeros((b,), dtype=jnp.float32)
        inp['adaptive_range'] = jnp.full((1,), 0.2, dtype=jnp.float32)
        return inp
    _L3_ffn_in = _L3_ffn_setup()
    _d = {'L0_attn_x': _L0_attn_in['x'], 'L0_attn_log_A': _L0_attn_in['log_A'], 'L0_attn_B_param': _L0_attn_in['B_param'], 'L0_attn_C_param': _L0_attn_in['C_param'], 'L0_attn_D_param': _L0_attn_in['D_param'], 'L0_attn_log_dt': _L0_attn_in['log_dt'], 'L0_attn_ln_gamma': _L0_attn_in['ln_gamma'], 'L0_attn_ln_beta': _L0_attn_in['ln_beta'], 'L0_attn_W_out': _L0_attn_in['W_out'], 'L0_attn_b_out': _L0_attn_in['b_out'], 'L0_ffn_ln_scale': _L0_ffn_in['ln_scale'], 'L0_ffn_ln_bias': _L0_ffn_in['ln_bias'], 'L0_ffn_gate_w': _L0_ffn_in['gate_w'], 'L0_ffn_Wg': _L0_ffn_in['Wg'], 'L0_ffn_Wu': _L0_ffn_in['Wu'], 'L0_ffn_Wd': _L0_ffn_in['Wd'], 'L0_ffn_sWg': _L0_ffn_in['sWg'], 'L0_ffn_sWu': _L0_ffn_in['sWu'], 'L0_ffn_sWd': _L0_ffn_in['sWd'], 'L1_attn_Wq': _L1_attn_in['Wq'], 'L1_attn_Wk': _L1_attn_in['Wk'], 'L1_attn_Wv': _L1_attn_in['Wv'], 'L1_attn_Wo': _L1_attn_in['Wo'], 'L1_attn_bo': _L1_attn_in['bo'], 'L1_ffn_w_gate': _L1_ffn_in['w_gate'], 'L1_ffn_w_up': _L1_ffn_in['w_up'], 'L1_ffn_w_down': _L1_ffn_in['w_down'], 'L2_attn_Wq': _L2_attn_in['Wq'], 'L2_attn_bq': _L2_attn_in['bq'], 'L2_attn_Wk': _L2_attn_in['Wk'], 'L2_attn_bk': _L2_attn_in['bk'], 'L2_attn_Wv': _L2_attn_in['Wv'], 'L2_attn_bv': _L2_attn_in['bv'], 'L2_attn_Wo': _L2_attn_in['Wo'], 'L2_attn_bo': _L2_attn_in['bo'], 'L2_ffn_w1_w': _L2_ffn_in['w1_w'], 'L2_ffn_w1_s': _L2_ffn_in['w1_s'], 'L2_ffn_w2_w': _L2_ffn_in['w2_w'], 'L2_ffn_w2_s': _L2_ffn_in['w2_s'], 'L2_ffn_h1_w': _L2_ffn_in['h1_w'], 'L2_ffn_h1_s': _L2_ffn_in['h1_s'], 'L2_ffn_h2_w': _L2_ffn_in['h2_w'], 'L2_ffn_h2_s': _L2_ffn_in['h2_s'], 'L2_ffn_w3_w': _L2_ffn_in['w3_w'], 'L2_ffn_w3_s': _L2_ffn_in['w3_s'], 'L3_attn_Wq': _L3_attn_in['Wq'], 'L3_attn_Wk': _L3_attn_in['Wk'], 'L3_attn_Wv': _L3_attn_in['Wv'], 'L3_attn_Wo': _L3_attn_in['Wo'], 'L3_ffn_cn_w1': _L3_ffn_in['cn_w1'], 'L3_ffn_cn_b1': _L3_ffn_in['cn_b1'], 'L3_ffn_cn_w2': _L3_ffn_in['cn_w2'], 'L3_ffn_cn_b2': _L3_ffn_in['cn_b2'], 'L3_ffn_cn_w3': _L3_ffn_in['cn_w3'], 'L3_ffn_cn_b3': _L3_ffn_in['cn_b3'], 'L3_ffn_cn_w4': _L3_ffn_in['cn_w4'], 'L3_ffn_cn_b4': _L3_ffn_in['cn_b4'], 'L3_ffn_gc_w1': _L3_ffn_in['gc_w1'], 'L3_ffn_gc_b1': _L3_ffn_in['gc_b1'], 'L3_ffn_gc_w2': _L3_ffn_in['gc_w2'], 'L3_ffn_gc_b2': _L3_ffn_in['gc_b2'], 'L3_ffn_gc_w3': _L3_ffn_in['gc_w3'], 'L3_ffn_gc_b3': _L3_ffn_in['gc_b3'], 'L3_ffn_adaptive_range': _L3_ffn_in['adaptive_range']}
    _x0 = _d['L0_attn_x']
    _d['L0_attn_x'] = jax.random.normal(jax.random.fold_in(jax.random.key(seed), 1), (16, 256, 128), dtype=_x0.dtype)
    del _x0
    return _d

def reference(L0_attn_x, L0_attn_log_A, L0_attn_B_param, L0_attn_C_param, L0_attn_D_param, L0_attn_log_dt, L0_attn_ln_gamma, L0_attn_ln_beta, L0_attn_W_out, L0_attn_b_out, L0_ffn_ln_scale, L0_ffn_ln_bias, L0_ffn_gate_w, L0_ffn_Wg, L0_ffn_Wu, L0_ffn_Wd, L0_ffn_sWg, L0_ffn_sWu, L0_ffn_sWd, L1_attn_Wq, L1_attn_Wk, L1_attn_Wv, L1_attn_Wo, L1_attn_bo, L1_ffn_w_gate, L1_ffn_w_up, L1_ffn_w_down, L2_attn_Wq, L2_attn_bq, L2_attn_Wk, L2_attn_bk, L2_attn_Wv, L2_attn_bv, L2_attn_Wo, L2_attn_bo, L2_ffn_w1_w, L2_ffn_w1_s, L2_ffn_w2_w, L2_ffn_w2_s, L2_ffn_h1_w, L2_ffn_h1_s, L2_ffn_h2_w, L2_ffn_h2_s, L2_ffn_w3_w, L2_ffn_w3_s, L3_attn_Wq, L3_attn_Wk, L3_attn_Wv, L3_attn_Wo, L3_ffn_cn_w1, L3_ffn_cn_b1, L3_ffn_cn_w2, L3_ffn_cn_b2, L3_ffn_cn_w3, L3_ffn_cn_b3, L3_ffn_cn_w4, L3_ffn_cn_b4, L3_ffn_gc_w1, L3_ffn_gc_b1, L3_ffn_gc_w2, L3_ffn_gc_b2, L3_ffn_gc_w3, L3_ffn_gc_b3, L3_ffn_adaptive_range):

    def _L0_attn_ref(x, log_A, B_param, C_param, D_param, log_dt, ln_gamma, ln_beta, W_out, b_out):
        import jax, jax.numpy as jnp
        import numpy as np
        BSZ, T, DM, N = (8, 512, 128, 64)
        LN_EPS = 1e-05
        residual = x
        mu = jnp.mean(x, axis=-1, keepdims=True)
        var = jnp.mean(jnp.square(x - mu), axis=-1, keepdims=True)
        xn = (x - mu) / jnp.sqrt(var + LN_EPS) * ln_gamma + ln_beta
        dt = jnp.exp(log_dt)
        dA = jnp.exp(-jnp.exp(log_A) * dt[:, None])
        dB = B_param * dt[:, None]

        def step(h, u):
            h = dA * h + dB * u[..., None]
            y = jnp.einsum('dn,bdn->bd', C_param, h) + D_param * u
            return (h, y)
        h0 = jnp.zeros((x.shape[0], x.shape[2], dA.shape[1]), x.dtype)
        _, ys = jax.lax.scan(step, h0, jnp.swapaxes(xn, 0, 1))
        y = jnp.swapaxes(ys, 0, 1)
        y = jnp.einsum('btd,ed->bte', y, W_out) + b_out
        return residual + y

    def _L0_ffn_ref(x, ln_scale, ln_bias, gate_w, Wg, Wu, Wd, sWg, sWu, sWd):
        import jax, jax.numpy as jnp
        import numpy as np
        EPS = 1e-05
        LN_EPS = 1e-05
        NUM_EXPERTS = 8
        TOP_K = 2
        HIDDEN = 128
        INTER = 256

        def _swiglu(x, wg, wu, wd):
            return jax.nn.silu(x @ wg) * (x @ wu) @ wd
        B, S, H = x.shape
        xf = x.reshape(-1, H)
        mu = jnp.mean(xf, axis=-1, keepdims=True)
        var = jnp.var(xf, axis=-1, keepdims=True)
        xn = (xf - mu) * jax.lax.rsqrt(var + LN_EPS) * ln_scale + ln_bias
        logits = xn @ gate_w.T
        probs = jax.nn.softmax(logits, axis=-1)
        tk_probs, tk_idx = jax.lax.top_k(probs, TOP_K)
        tk_probs = tk_probs / (jnp.sum(tk_probs, axis=-1, keepdims=True) + EPS)
        onehot = tk_idx[..., None] == jnp.arange(NUM_EXPERTS)[None, None, :]
        w = jnp.sum(tk_probs[..., None] * onehot.astype(tk_probs.dtype), axis=1)
        out = _swiglu(xf, sWg, sWu, sWd)
        for e in range(NUM_EXPERTS):
            out = out + w[:, e:e + 1] * _swiglu(xf, Wg[e], Wu[e], Wd[e])
        return out.reshape(B, S, H)

    def _L1_attn_ref(x, Wq, Wk, Wv, Wo, bo):
        import jax, jax.numpy as jnp
        import numpy as np
        B, S, D_IN, D_OUT, H = (4, 256, 128, 128, 16)
        HD = D_OUT // H
        b, s, _ = x.shape

        def split_heads(t):
            return t.reshape(b, s, H, HD).transpose(0, 2, 1, 3)
        q = split_heads(x @ Wq)
        k = split_heads(x @ Wk)
        v = split_heads(x @ Wv)
        scores = jnp.einsum('bhqd,bhkd->bhqk', q, k)
        causal = jnp.triu(jnp.ones((s, s), dtype=bool), k=1)
        scores = jnp.where(causal, -jnp.inf, scores)
        attn = jax.nn.softmax(scores / np.sqrt(HD), axis=-1)
        ctx = jnp.einsum('bhqk,bhkd->bhqd', attn, v)
        ctx = ctx.transpose(0, 2, 1, 3).reshape(b, s, D_OUT)
        return ctx @ Wo + bo

    def _L1_ffn_ref(x, w_gate, w_up, w_down):
        import jax, jax.numpy as jnp
        import numpy as np
        DIM = 128
        HIDDEN = 384
        SCALE = 1.0 / 127.0

        def _dequant(w_int, dtype):
            return w_int.astype(dtype) * jnp.asarray(SCALE, dtype)
        wg = _dequant(w_gate, x.dtype)
        wu = _dequant(w_up, x.dtype)
        wd = _dequant(w_down, x.dtype)
        gate = jnp.einsum('bsd,hd->bsh', x, wg)
        up = jnp.einsum('bsd,hd->bsh', x, wu)
        h = jax.nn.silu(gate) * up
        return jnp.einsum('bsh,dh->bsd', h, wd)

    def _L2_attn_ref(x, Wq, bq, Wk, bk, Wv, bv, Wo, bo):
        import jax, jax.numpy as jnp
        import numpy as np
        N_EMBD = 128
        N_HEAD = 16
        HEAD_SIZE = N_EMBD // N_HEAD
        WINDOW = 3

        def _shift(a, j):
            if j == 0:
                return a
            return jnp.pad(a, ((0, 0), (0, 0), (j, 0), (0, 0)))[:, :, :-j, :]
        B, T, C = x.shape
        H, d = (N_HEAD, HEAD_SIZE)
        scale = 1.0 / np.sqrt(d)
        q = (x @ Wq.T + bq).reshape(B, T, H, d).transpose(0, 2, 1, 3)
        k = (x @ Wk.T + bk).reshape(B, T, H, d).transpose(0, 2, 1, 3)
        v = (x @ Wv.T + bv).reshape(B, T, H, d).transpose(0, 2, 1, 3)
        scores = jnp.stack([jnp.einsum('bhtd,bhtd->bht', q, _shift(k, j)) * scale for j in range(WINDOW)], axis=-1)
        valid = jnp.arange(T)[:, None] >= jnp.arange(WINDOW)[None, :]
        scores = jnp.where(valid[None, None], scores, -jnp.inf)
        att = jax.nn.softmax(scores, axis=-1)
        y = sum((att[..., j:j + 1] * _shift(v, j) for j in range(WINDOW)))
        y = y.transpose(0, 2, 1, 3).reshape(B, T, C)
        return y @ Wo.T + bo

    def _L2_ffn_ref(x, w1_w, w1_s, w2_w, w2_s, h1_w, h1_s, h2_w, h2_s, w3_w, w3_s):
        import jax, jax.numpy as jnp
        import numpy as np
        D_IN, D_HID = (128, 512)

        def _ternary(key, shape):
            return jax.random.randint(key, shape, -1, 2).astype(jnp.float32)

        def _tlin(x, w, s):
            return jnp.einsum('bsi,oi->bso', x, w) * s
        h = jax.nn.silu(_tlin(x, w1_w, w1_s)) * _tlin(x, w2_w, w2_s)
        h = jax.nn.gelu(_tlin(h, h1_w, h1_s), approximate=False)
        h = jax.nn.gelu(_tlin(h, h2_w, h2_s), approximate=False)
        return _tlin(h, w3_w, w3_s)

    def _L3_attn_ref(x, Wq, Wk, Wv, Wo):
        import jax, jax.numpy as jnp
        import numpy as np
        from math import sqrt
        EMBED_DIM = 128
        NUM_HEADS = 16
        HEAD_DIM = EMBED_DIM // NUM_HEADS
        CAUSAL = True
        B, S, E = x.shape
        H, D = (NUM_HEADS, HEAD_DIM)

        def proj(W):
            y = jnp.einsum('bse,fe->bsf', x, W)
            return y.reshape(B, S, H, D).transpose(0, 2, 1, 3)
        q, k, v = (proj(Wq), proj(Wk), proj(Wv))
        scores = jnp.einsum('bhsd,bhtd->bhst', q, k)
        if CAUSAL:
            mask = jnp.triu(jnp.ones((S, S), dtype=bool), k=1)
            scores = jnp.where(mask, -jnp.inf, scores)
        attn = jax.nn.softmax(scores / sqrt(D), axis=-1)
        out = jnp.einsum('bhst,bhtd->bhsd', attn, v)
        out = out.transpose(0, 2, 1, 3).reshape(B, S, E)
        return jnp.einsum('bse,fe->bsf', out, Wo)

    def _L3_ffn_ref(x, cn_w1, cn_b1, cn_w2, cn_b2, cn_w3, cn_b3, cn_w4, cn_b4, gc_w1, gc_b1, gc_w2, gc_b2, gc_w3, gc_b3, adaptive_range):
        import jax, jax.numpy as jnp
        import numpy as np
        B, S, DIM = (4, 512, 128)
        BASE_COUPLING = 0.1
        NUM_CYCLES = 3

        def _gelu(x):
            return jax.nn.gelu(x, approximate=False)

        def _coupling_net(h, w1, b1, w2, b2, w3, b3, w4, b4):
            h = _gelu(h @ w1 + b1)
            h = _gelu(h @ w2 + b2)
            h = _gelu(h @ w3 + b3)
            return jax.nn.sigmoid(h @ w4 + b4)

        def _global_net(h, w1, b1, w2, b2, w3, b3):
            h = _gelu(h @ w1 + b1)
            h = _gelu(h @ w2 + b2)
            return jax.nn.sigmoid(h @ w3 + b3)

        def _twist(x):
            o_r, o_i, p_r, p_i = jnp.split(x, 4, axis=-1)
            return jnp.concatenate([p_r, -p_i, -o_r, o_i], axis=-1)
        global_context = x.mean(axis=1, keepdims=True)
        gf = _global_net(global_context, gc_w1, gc_b1, gc_w2, gc_b2, gc_w3, gc_b3)
        out = x
        for _ in range(NUM_CYCLES):
            tf = _coupling_net(out, cn_w1, cn_b1, cn_w2, cn_b2, cn_w3, cn_b3, cn_w4, cn_b4)
            combined = 0.7 * gf + 0.3 * tf
            coupling = BASE_COUPLING + adaptive_range * (combined - 0.5) * 2.0
            out = out + coupling * _twist(out)
        return out
    x = L0_attn_x
    xn = _layernorm(x, axis=-1)
    x = x + _L0_attn_ref(xn, L0_attn_log_A, L0_attn_B_param, L0_attn_C_param, L0_attn_D_param, L0_attn_log_dt, L0_attn_ln_gamma, L0_attn_ln_beta, L0_attn_W_out, L0_attn_b_out) + _L0_ffn_ref(xn, L0_ffn_ln_scale, L0_ffn_ln_bias, L0_ffn_gate_w, L0_ffn_Wg, L0_ffn_Wu, L0_ffn_Wd, L0_ffn_sWg, L0_ffn_sWu, L0_ffn_sWd)
    xn = _layernorm(x, axis=-1)
    x = x + _L1_attn_ref(xn, L1_attn_Wq, L1_attn_Wk, L1_attn_Wv, L1_attn_Wo, L1_attn_bo) + _L1_ffn_ref(xn, L1_ffn_w_gate, L1_ffn_w_up, L1_ffn_w_down)
    xn = _layernorm(x, axis=-1)
    x = x + _L2_attn_ref(xn, L2_attn_Wq, L2_attn_bq, L2_attn_Wk, L2_attn_bk, L2_attn_Wv, L2_attn_bv, L2_attn_Wo, L2_attn_bo) + _L2_ffn_ref(xn, L2_ffn_w1_w, L2_ffn_w1_s, L2_ffn_w2_w, L2_ffn_w2_s, L2_ffn_h1_w, L2_ffn_h1_s, L2_ffn_h2_w, L2_ffn_h2_s, L2_ffn_w3_w, L2_ffn_w3_s)
    xn = _layernorm(x, axis=-1)
    x = x + _L3_attn_ref(xn, L3_attn_Wq, L3_attn_Wk, L3_attn_Wv, L3_attn_Wo) + _L3_ffn_ref(xn, L3_ffn_cn_w1, L3_ffn_cn_b1, L3_ffn_cn_w2, L3_ffn_cn_b2, L3_ffn_cn_w3, L3_ffn_cn_b3, L3_ffn_cn_w4, L3_ffn_cn_b4, L3_ffn_gc_w1, L3_ffn_gc_b1, L3_ffn_gc_w2, L3_ffn_gc_b2, L3_ffn_gc_w3, L3_ffn_gc_b3, L3_ffn_adaptive_range)
    return x

_drawn_inputs = setup_inputs


def setup_inputs(seed=0):
    import zlib

    import numpy as np

    out = dict(_drawn_inputs(seed))
    spreads = {'L0_attn_D_param': (1.0, 0.2),
     'L0_attn_ln_gamma': (1.0, 0.2),
     'L0_attn_ln_beta': (0.0, 0.1),
     'L0_attn_b_out': (0.0, 0.1),
     'L0_ffn_ln_scale': (1.0, 0.2),
     'L0_ffn_ln_bias': (0.0, 0.1),
     'L3_ffn_cn_b1': (0.0, 0.1),
     'L3_ffn_cn_b2': (0.0, 0.1),
     'L3_ffn_cn_b3': (0.0, 0.1),
     'L3_ffn_gc_b1': (0.0, 0.1),
     'L3_ffn_gc_b2': (0.0, 0.1)}
    factors = {}
    for name, (base, spread) in spreads.items():
        noise = np.random.default_rng([zlib.crc32(name.encode()), seed]).standard_normal(out[name].shape)
        drawn = base * np.exp(spread * noise) if base else spread * noise
        out[name] = jnp.asarray(drawn.astype(out[name].dtype))
    for name, factor in factors.items():
        out[name] = (out[name] * factor).astype(out[name].dtype)
    return out
```

```python
from contextlib import ExitStack

import concourse.bass as bass
from concourse import mybir

F32 = mybir.dt.float32
F16 = mybir.dt.float16
I32 = mybir.dt.int32
ALU = mybir.AluOpType
ACT = mybir.ActivationFunctionType
AX = mybir.AxisListType

P = 128
BATCH, SEQ, DM = 16, 256, 128
TILES = BATCH * SEQ // P
CHUNK = 512
NCH = BATCH * SEQ // CHUNK
TPC = CHUNK // P
NST = 64
NE = 8
INTER = 256
IT = INTER // P
HEADS, HD = 16, 8
NG = 4
EPS = 1e-5
MASKED = -60000.0


def sl(i, n):
    return bass.ds(i, n)


def spread(ap, dims):
    return bass.AP(tensor=ap.tensor, offset=ap.offset, ap=[list(ap.ap[0])] + dims)


class Program:

    def __init__(self, nc, ctx, dram, out):
        self.nc, self.ctx, self.dram, self.out = nc, ctx, dram, out

        self.stage_sems = ExitStack()
        self.used = []

    def sem(self, name):
        s = self.stage_sems.enter_context(self.nc.semaphore(name))
        self.used.append(s)
        return s

    def end_layer(self):
        with self.nc.Block() as block:

            @block.gpsimd
            def _(pool):
                for s in self.used:
                    pool.sem_clear(s)

        self.stage_sems.close()
        self.used = []

    def sb(self, name, shape, dt=F32, ctx=None):
        return (ctx or self.ctx).enter_context(self.nc.sbuf_tensor(name, shape, dt))



def load(k):
    nc, d = k.nc, k.dram
    arrived = k.sem("inputs_arrived")
    cleared = k.sem("constants_cleared")
    loads = [(k.x[:], d["L0_attn_x"].rearrange("b (h p) d -> p (b h) d", p=P))] + k.loads
    k.loads = []
    with nc.Block() as block:

        @block.sync
        def _(sp):
            for dst, src in loads:
                sp.dma_start(dst, src).then_inc(arrived, 16)
            sp.wait_ge(arrived, 16 * len(loads))

        @block.gpsimd
        def _(pool):
            pool.memset(k.ident[:], 0.0).then_inc(cleared, 1)
            pool.memset(k.ident16[:], 0.0).then_inc(cleared, 1)
            pool.memset(k.mask_kq[:], 0.0).then_inc(cleared, 1)
            pool.memset(k.mask_qk[:], 0.0).then_inc(cleared, 1)
            pool.memset(k.eps[:], EPS).then_inc(cleared, 1)
            pool.iota(k.lag_i[:], pattern=[[1, SEQ]], base=0, channel_multiplier=0).then_inc(cleared, 1)
            pool.memset(k.mirror[:], 0.0).then_inc(cleared, 1)
            pool.wait_ge(cleared, 7)
            pool.affine_select(out=k.mirror[:], in_=k.mirror[:], compare_op=ALU.not_equal, fill=1.0, base=1 - P,
                               pattern=[[1, P]], channel_multiplier=1)
            for m in (k.ident, k.ident16):
                pool.affine_select(out=m[:], in_=m[:], compare_op=ALU.not_equal, fill=1.0, base=0,
                                   pattern=[[-1, P]], channel_multiplier=1)
            pool.affine_select(out=k.mask_kq[:], in_=k.mask_kq[:], compare_op=ALU.is_ge, fill=MASKED,
                               base=0, pattern=[[0, 4], [1, P]], channel_multiplier=-1)
            pool.affine_select(out=k.mask_qk[:], in_=k.mask_qk[:], compare_op=ALU.is_ge, fill=MASKED,
                               base=0, pattern=[[0, 4], [-1, P]], channel_multiplier=1)
            pool.tensor_copy(k.lag[:], k.lag_i[:])

        @block.vector
        def _(dve):
            dve.memset(k.ps[:], 0.0)



def norm(k, tag, src, chan, z_out=None, loads=()):
    nc = k.nc
    stats_done, aggr_done, std_done = k.sem(f"{tag}_stats"), k.sem(f"{tag}_aggr"), k.sem(f"{tag}_std")
    rstd_done, z_ready, turned = k.sem(f"{tag}_rstd"), k.sem(f"{tag}_z"), k.sem(f"{tag}_turned")
    bank_free = k.sem(f"{tag}_bank_free")
    st, mv, std, rstd, z = k.st, k.mv, k.std, k.rstd, k.z8
    RING = 8
    with nc.Block() as block:

        @block.sync
        def _(sp):
            for arrived, weights in loads:
                for dst, from_dram in weights:
                    sp.dma_start(dst, from_dram).then_inc(arrived, 16)

        @block.vector
        def _(dve):
            with dve.Fori(0, TILES // 4) as i:
                for m in range(4):
                    dve.bn_stats(st[:, sl(i * 4 + m, 1), :], src[:, sl(i * 4 + m, 1), :]).then_inc(stats_done, 1)
            dve.wait_ge(stats_done, TILES)
            for t in range(TILES):
                dve.bn_aggr(mv[:, t, :], st[:, t, :]).then_inc(aggr_done, 1)
            dve.wait_ge(std_done, 1)
            dve.reciprocal(rstd[:], std[:]).then_inc(rstd_done, 1)
            dve.wait_ge(rstd_done, 1)
            with dve.Fori(0, TILES // RING) as i:
                for m in range(RING):
                    t = i * RING + m
                    if z_out is not None:
                        dve.tensor_scalar(z_out[:, sl(t, 1), :], src[:, sl(t, 1), :], mv[:, sl(t, 1), 0:1],
                                          rstd[:, sl(t, 1)], ALU.subtract, ALU.mult)
                    dve.wait_ge(turned, t + 1)
                    dve.tensor_scalar(z[:, m, :], src[:, sl(t, 1), :], mv[:, sl(t, 1), 0:1],
                                      rstd[:, sl(t, 1)], ALU.subtract, ALU.mult).then_inc(z_ready, 1)

        @block.scalar
        def _(act):
            act.wait_ge(aggr_done, TILES)
            act.activation(std[:], mv[:, :, 1], ACT.Sqrt, bias=k.eps[:, 0:1]).then_inc(std_done, 1)
            act.sem_inc(bank_free, 2)
            with act.Fori(0, TILES // RING) as i:
                for m in range(2):
                    act.wait_ge(turned, RING + i * RING + 4 * m + 4)
                    act.activation(chan[:, sl(i * 2 * CHUNK + m * CHUNK, CHUNK)], k.ps[:, m, :],
                                   ACT.Copy).then_inc(bank_free, 1)

        @block.tensor
        def _(pe):
            pe.sem_inc(turned, RING)
            with pe.Fori(0, TILES // RING) as i:
                for m in range(RING):
                    if m % 4 == 0:
                        pe.wait_ge(bank_free, i * 2 + m // 4 + 1)
                    pe.wait_ge(z_ready, i * RING + m + 1)
                    pe.transpose(k.ps[:, m // 4, m % 4 * P:m % 4 * P + P], z[:, m, :],
                                 k.ident[:]).then_inc(turned, 1)



def gates(k, zT, weight):
    nc = k.nc
    g_ready, logits_done = k.sem("gate_in"), k.sem("gate_logits")
    step = k.sem("gate_step")
    exped = k.sem("gate_exp")
    with ExitStack() as st, nc.Block() as block:
        g = k.sb("gate_g", [P, 2, CHUNK], ctx=st)
        lg = k.ps[:, 7, 0:TILES * NE].rearrange("p (t e) -> p t e", e=NE)
        pr = k.sb("gate_p", [P, TILES, NE], ctx=st)
        red = k.sb("gate_red", [P, TILES], ctx=st)
        inv = k.sb("gate_inv", [P, TILES], ctx=st)
        cmp1 = k.sb("gate_cmp1", [P, TILES, NE, NE], ctx=st)
        cmp2 = k.sb("gate_cmp2", [P, TILES, NE, NE], ctx=st)
        earlier = k.sb("gate_earlier", [P, NE, NE], ctx=st)
        made = k.sem("gate_earlier_made")

        @block.gpsimd
        def _(pool):
            pool.memset(earlier[:], 1.0).then_inc(made, 1)
            pool.wait_ge(made, 1)
            pool.affine_select(out=earlier[:], in_=earlier[:], compare_op=ALU.is_gt, fill=0.0, base=0,
                               pattern=[[1, NE], [-1, NE]], channel_multiplier=0).then_inc(made, 1)

        @block.scalar
        def _(act):
            with act.Fori(0, NCH // 2) as i:
                for m in range(2):
                    act.wait_ge(logits_done, i * 2 + m + 1)
                    act.activation(g[:, m, :], zT[:, sl(i * 2 * CHUNK + m * CHUNK, CHUNK)], ACT.Identity,
                                   scale=k.w["ffn_scale"][:, 0:1], bias=k.w["ffn_bias"][:, 0:1]).then_inc(g_ready, 1)
            act.wait_ge(step, 2)
            act.activation(pr[:], pr[:], ACT.Exp).then_inc(exped, 1)

        @block.tensor
        def _(pe):
            pe.sem_inc(logits_done, 2)
            for c in range(NCH):
                pe.wait_ge(g_ready, c + 1)
                for t in range(TPC):
                    ins = pe.matmul(lg[:, c * TPC + t, :], g[:, c % 2, t * P:t * P + P], k.w["gate"][:],
                                    start=True, stop=True)
                ins.then_inc(logits_done, 1)

        @block.vector
        def _(dve):
            n = 0

            def link(ins):
                nonlocal n
                n += 1
                ins.then_inc(step, 1)
                dve.wait_ge(step, n)

            def rows(a):
                return a[:].unsqueeze(2).to_broadcast([P, TILES, NE])

            dve.wait_ge(logits_done, NCH + 2)
            link(dve.tensor_reduce(red[:], lg, AX.X, ALU.max))
            link(dve.tensor_tensor(pr[:], lg, rows(red), ALU.subtract))
            dve.wait_ge(exped, 1)
            dve.wait_ge(made, 2)
            link(dve.tensor_reduce(red[:], pr[:], AX.X, ALU.add))
            link(dve.reciprocal(inv[:], red[:]))
            link(dve.tensor_tensor(pr[:], pr[:], rows(inv), ALU.mult))
            own = pr[:].unsqueeze(3).to_broadcast([P, TILES, NE, NE])
            other = pr[:].unsqueeze(2).to_broadcast([P, TILES, NE, NE])
            dve.tensor_tensor(cmp1[:], other, own, ALU.is_gt)
            link(dve.tensor_tensor(cmp2[:], other, own, ALU.is_equal))
            link(dve.tensor_tensor(cmp2[:], cmp2[:], earlier[:].unsqueeze(1).to_broadcast([P, TILES, NE, NE]),
                                   ALU.mult))
            link(dve.tensor_tensor(cmp1[:], cmp1[:], cmp2[:], ALU.add))
            link(dve.tensor_reduce(weight[:], cmp1[:], AX.X, ALU.add))
            link(dve.scalar_tensor_tensor(out=pr[:], in0=weight[:], scalar=1.5, in1=pr[:], op0=ALU.is_lt,
                                          op1=ALU.mult))
            link(dve.tensor_reduce(red[:], pr[:], AX.X, ALU.add))
            link(dve.tensor_scalar(red[:], red[:], EPS, None, ALU.add))
            link(dve.reciprocal(inv[:], red[:]))
            link(dve.tensor_tensor(weight[:], pr[:], rows(inv), ALU.mult))



def ssm_kernel(k, zz, u):
    nc, w = k.nc, k.w
    step, exps, e_ready, e_used = k.sem("ssm_step"), k.sem("ssm_pre"), k.sem("ssm_e"), k.sem("ssm_e_used")
    stored, zeroed = k.sem("ssm_stored"), k.sem("ssm_zeroed")
    u_step, u_mirrored, u_stored = k.sem("ssm_u"), k.sem("ssm_u_mirrored"), k.sem("ssm_u_stored")
    NU = 2 * DM * BATCH // CHUNK
    flat = u[:].rearrange("p h d b -> p (h d b)")
    with ExitStack() as st, nc.Block() as block:
        dt = k.sb("ssm_dt", [P, 1], ctx=st)
        ea = k.sb("ssm_ea", [P, NST], ctx=st)
        nr = k.sb("ssm_nr", [P, NST], ctx=st)
        cb = k.sb("ssm_cb", [P, NST], ctx=st)
        e = k.sb("ssm_e", [P, 4, SEQ], ctx=st)
        kn = k.sb("ssm_k", [P, 4, SEQ], ctx=st)
        zero = k.sb("ssm_zero", [P, P], ctx=st)

        @block.scalar
        def _(act):
            act.activation(dt[:], w["log_dt"][:], ACT.Exp).then_inc(exps, 1)
            act.activation(ea[:], w["log_A"][:], ACT.Exp).then_inc(exps, 1)
            act.wait_ge(step, 2)
            with act.Fori(0, NST // 4) as i:
                for m in range(4):
                    act.wait_ge(e_used, i * 4 + m + 1)
                    act.activation(e[:, m, :], k.lag[:], ACT.Exp, scale=nr[:, sl(i * 4 + m, 1)]).then_inc(e_ready, 1)
            for c in range(NU):
                act.wait_ge(u_mirrored, c + 1)
                act.activation(flat[:, c * CHUNK:(c + 1) * CHUNK], k.ps[:, c, :], ACT.Copy).then_inc(u_stored, 1)
            act.wait_ge(u_stored, NU)

        @block.tensor
        def _(pe):
            for c in range(NU):
                pe.wait_ge(u_step, 2 if c < NU // 2 else 4)
                pe.matmul(k.ps[:, c, :], k.mirror[:], flat[:, c * CHUNK:(c + 1) * CHUNK],
                          start=True, stop=True).then_inc(u_mirrored, 1)

        @block.gpsimd
        def _(pool):
            pool.memset(zero[:], 0.0).then_inc(zeroed, 1)
            ga = w["gamma"][:].unsqueeze(1).to_broadcast([P, BATCH, DM])
            be = w["beta"][:].unsqueeze(1).to_broadcast([P, BATCH, DM])
            for h in range(2):
                src = zz[:].rearrange("p (b h) d -> p b h d", h=2)[:, :, h, :]
                pool.tensor_tensor(src, src, ga, ALU.mult).then_inc(u_step, 1)
                pool.wait_ge(u_step, 2 * h + 1)
                pool.tensor_tensor(u[:, h].rearrange("p d b -> p b d"), src, be, ALU.add).then_inc(u_step, 1)

        @block.vector
        def _(dve):
            dve.wait_ge(exps, 2)
            dve.tensor_scalar(nr[:], ea[:], dt[:, 0:1], -1.0, ALU.mult, ALU.mult).then_inc(step, 1)
            dve.scalar_tensor_tensor(out=cb[:], in0=w["B"][:], scalar=dt[:, 0:1], in1=w["C"][:],
                                     op0=ALU.mult, op1=ALU.mult).then_inc(step, 1)
            dve.memset(kn[:], 0.0).then_inc(step, 1)
            dve.wait_ge(step, 3)
            dve.sem_inc(e_used, 4)
            with dve.Fori(0, NST // 4) as i:
                for m in range(4):
                    dve.wait_ge(e_ready, i * 4 + m + 1)
                    dve.wait_ge(e_used, i * 4 + m + 1)
                    dve.scalar_tensor_tensor(out=kn[:, m, :], in0=e[:, m, :], scalar=cb[:, sl(i * 4 + m, 1)],
                                             in1=kn[:, m, :], op0=ALU.mult, op1=ALU.add).then_inc(e_used, 1)
            dve.wait_ge(e_used, NST + 4)
            dve.tensor_tensor(kn[:, 0:2, :], kn[:, 0:2, :], kn[:, 2:4, :], ALU.add).then_inc(step, 1)
            dve.wait_ge(step, 4)
            dve.tensor_tensor(kn[:, 0, :], kn[:, 0, :], kn[:, 1, :], ALU.add).then_inc(step, 1)
            dve.wait_ge(step, 5)
            dve.tensor_tensor(kn[:, 0, 0:1], kn[:, 0, 0:1], w["D"][:], ALU.add).then_inc(step, 1)

        @block.sync
        def _(sp):
            sp.wait_ge(zeroed, 1)
            sp.dma_start(k.kpad[:, 0:P], zero[:]).then_inc(stored, 16)
            sp.wait_ge(step, 6)
            sp.dma_start(k.kpad[:, P:P + SEQ], kn[:, 0, :]).then_inc(stored, 16)
            sp.wait_ge(stored, 32)


def convolve(k, u):
    nc = k.nc
    t_in = [k.sem(f"conv_toeplitz{m}") for m in range(2)]
    u_copied, used = k.sem("conv_u"), k.sem("conv_used")
    y_free, stored = k.sem("conv_y_free"), [k.sem(f"conv_stored{m}") for m in range(2)]
    CH = 8
    STEPS = DM // CH
    yv = k.yT.rearrange("(s g j) b t -> s j b g t", g=2, j=4)
    with ExitStack() as st, nc.Block() as block:
        toe = k.sb("toeplitz", [P, 2, CH, SEQ], ctx=st)
        uc = k.sb("conv_uc", [P, 2, 2, CH, BATCH], ctx=st)
        y = k.sb("conv_ysb", [P, 2, 2, SEQ], ctx=st)

        @block.sync
        def _(sp):
            with sp.Fori(0, STEPS // 2) as i:
                for m in range(2):
                    s = i * 2 + m
                    sp.wait_ge(used, s + 1)
                    src = bass.AP(tensor=k.kpad.tensor, offset=s * (CH * (P + SEQ)) + 1,
                                  ap=[[1, P], [P + SEQ, CH], [1, SEQ]])
                    sp.dma_start(toe[:, m], src).then_inc(t_in[m], 16)

        @block.gpsimd
        def _(pool):
            with pool.Fori(0, STEPS // 2) as i:
                for m in range(2):
                    s = i * 2 + m
                    pool.wait_ge(used, s + 1)
                    pool.tensor_copy(uc[:, m], u[:, :, sl(s * CH, CH), :]).then_inc(u_copied, 1)

        @block.tensor
        def _(pe):
            pe.sem_inc(used, 2)
            with pe.Fori(0, STEPS // 2) as i:
                for m in range(2):
                    s = i * 2 + m
                    pe.wait_ge(t_in[m], i * 16 + 16)
                    pe.wait_ge(u_copied, s + 1)
                    pe.wait_ge(y_free, s + 1)
                    for c in range(CH):
                        g, j = c // 4, c % 4
                        o = k.ps[32 * j:32 * j + BATCH, m, g * SEQ:g * SEQ + SEQ]
                        pe.matmul(o, uc[:, m, 0, c, :], toe[:, m, c, :], start=True, stop=False,
                                  skip_group_check=True)
                        ins = pe.matmul(o[:, P:SEQ], uc[:, m, 1, c, :], toe[:, m, c, 0:P], start=False, stop=True,
                                        skip_group_check=True)
                    ins.then_inc(used, 1)

        @block.vector
        def _(dve):
            dve.sem_inc(y_free, 2)
            with dve.Fori(0, STEPS // 2) as i:
                for m in range(2):
                    s = i * 2 + m
                    dve.wait_ge(used, s + 3)
                    dve.wait_ge(stored[m], i * 64 + 64)
                    dve.tensor_copy(y[:, m].rearrange("p g t -> p (g t)"), k.ps[:, m, :]).then_inc(y_free, 1)

        @block.scalar
        def _(act):
            for m in range(2):
                act.sem_inc(stored[m], 64)
            with act.Fori(0, STEPS // 2) as i:
                for m in range(2):
                    s = i * 2 + m
                    act.wait_ge(y_free, s + 3)
                    for j in range(4):
                        act.dma_start(yv[sl(s, 1), j], y[32 * j:32 * j + BATCH, m]).then_inc(stored[m], 16)
            for m in range(2):
                act.wait_ge(stored[m], 64 + STEPS // 2 * 64)



def experts(k, xT, weight):
    nc, w = k.nc, k.w
    PAIRS, N = (NE + 1) * IT, NE + 1
    gate_mm, up_mm, sg_ready, h_ready = k.sem("ex_gate"), k.sem("ex_up"), k.sem("ex_silu"), k.sem("ex_h")
    down_mm, acc_done, y_in, y_used = k.sem("ex_down"), k.sem("ex_acc"), k.sem("ex_y"), k.sem("ex_y_used")
    GB, UB, OB = (0, 1), (2, 3), (4, 5, 6)
    with ExitStack() as st, nc.Block() as block:
        sg = k.sb("ex_sg", [P, 2, CHUNK], ctx=st)
        h = k.sb("ex_h_sb", [P, 3, IT, CHUNK], ctx=st)
        y = k.sb("ex_y_sb", [P, CHUNK], ctx=st)

        @block.sync
        def _(sp):
            with sp.Fori(0, NCH) as i:
                sp.wait_ge(y_used, i + 1)
                sp.dma_start(y[:].rearrange("d (b t) -> d b t", b=2), k.yT[:, sl(i * 2, 2), :]).then_inc(y_in, 16)

        @block.tensor
        def _(pe):
            pe.sem_inc(y_used, 1)
            with pe.Fori(0, NCH) as i:
                def gate_up(e):
                    for it in range(IT):
                        n = e * IT + it
                        xc = xT[:, sl(i * CHUNK, CHUNK)]
                        pe.wait_ge(sg_ready, i * PAIRS + n + 1)
                        pe.matmul(k.ps[:, GB[n % 2], :], w["Wg"][:, e, it * P:it * P + P], xc,
                                  start=True, stop=True).then_inc(gate_mm, 1)
                        pe.wait_ge(h_ready, i * PAIRS + n + 1)
                        pe.matmul(k.ps[:, UB[n % 2], :], w["Wu"][:, e, it * P:it * P + P], xc,
                                  start=True, stop=True).then_inc(up_mm, 1)

                def down(e):
                    pe.wait_ge(acc_done, i * N + e + 1)
                    if e == NE:
                        pe.wait_ge(y_in, i * 16 + 16)
                        for t in range(TPC):
                            ins = pe.matmul(k.ps[:, OB[e % 3], t * P:t * P + P], y[:, t * P:t * P + P],
                                            w["W_out"][:], start=(t == 0), stop=False, skip_group_check=True)
                        ins.then_inc(y_used, 1)
                    pe.wait_ge(h_ready, 2 + i * PAIRS + (e + 1) * IT)
                    for t in range(TPC):
                        for it in range(IT):
                            ins = pe.matmul(k.ps[:, OB[e % 3], t * P:t * P + P], h[:, e % 3, it, t * P:t * P + P],
                                            w["Wd"][:, e, it, :], start=(it == 0 and e < NE), stop=(it == IT - 1),
                                            skip_group_check=True)
                    ins.then_inc(down_mm, 1)

                for e in range(N):
                    gate_up(e)
                    if e:
                        down(e - 1)
                down(NE)

        @block.scalar
        def _(act):
            act.sem_inc(sg_ready, 2)
            with act.Fori(0, NCH) as i:
                for n in range(PAIRS):
                    act.wait_ge(gate_mm, i * PAIRS + n + 1)
                    act.wait_ge(h_ready, i * PAIRS + n + 1)
                    act.activation(sg[:, n % 2, :], k.ps[:, GB[n % 2], :], ACT.Silu).then_inc(sg_ready, 1)

        @block.vector
        def _(dve):
            dve.sem_inc(h_ready, 2)
            dve.sem_inc(acc_done, 3)
            with dve.Fori(0, NCH) as i:
                def gated(e):
                    dve.wait_ge(acc_done, i * N + e + 1)
                    for it in range(IT):
                        n = e * IT + it
                        dve.wait_ge(sg_ready, 2 + i * PAIRS + n + 1)
                        dve.wait_ge(up_mm, i * PAIRS + n + 1)
                        dve.tensor_tensor(h[:, e % 3, it, :], sg[:, n % 2, :], k.ps[:, UB[n % 2], :],
                                          ALU.mult).then_inc(h_ready, 1)

                def add(e):
                    dve.wait_ge(down_mm, i * N + e + 1)
                    dve.wait_ge(acc_done, i * N + e + 3)
                    if e < NE:
                        for t in range(TPC):
                            T = i * TPC + t
                            xt = k.x[:, sl(T, 1), :]
                            ins = dve.scalar_tensor_tensor(
                                out=xt, in0=k.ps[:, OB[e % 3], t * P:t * P + P].unsqueeze(1),
                                scalar=weight[:, sl(T, 1), e:e + 1].rearrange("p a b -> p (a b)"), in1=xt,
                                op0=ALU.mult, op1=ALU.add)
                    else:
                        xc = k.x[:, sl(i * TPC, TPC), :]
                        ins = dve.tensor_tensor(xc, xc, k.ps[:, OB[e % 3], :].rearrange("p (t c) -> p t c", c=P),
                                                ALU.add)
                    ins.then_inc(acc_done, 1)

                for e in range(N):
                    gated(e)
                    if e > 1:
                        add(e - 2)
                add(N - 2)
                add(N - 1)




ROWS = 4


def project(k, tag, xT, wq, wk, wv, bo):
    nc = k.nc
    x_copied, qk_mm, v_mm = k.sem(f"{tag}_xc"), k.sem(f"{tag}_qk"), k.sem(f"{tag}_v")
    hi_done, lo_done, v_done = k.sem(f"{tag}_hi"), k.sem(f"{tag}_lo"), k.sem(f"{tag}_vd")
    stored, const_set, const_stored = k.sem(f"{tag}_st"), k.sem(f"{tag}_cs"), k.sem(f"{tag}_cst")
    with ExitStack() as st, nc.Block() as block:
        xc = k.sb(f"{tag}_x", [P, CHUNK], ctx=st)
        hi = k.sb(f"{tag}_hi_sb", [P, 2, CHUNK], F16, ctx=st)
        lo = k.sb(f"{tag}_lo_sb", [P, 2, CHUNK], F16, ctx=st)
        const = k.sb(f"{tag}_const", [P, 2, SEQ], F16, ctx=st)

        @block.gpsimd
        def _(pool):
            pool.memset(const[:, 0, :], 0.0).then_inc(const_set, 1)
            pool.memset(const[:, 1, :], 1.0).then_inc(const_set, 1)
            with pool.Fori(0, NCH) as i:
                pool.wait_ge(v_mm, i + 1)
                pool.tensor_copy(xc[:], xT[:, sl(i * CHUNK, CHUNK)]).then_inc(x_copied, 1)
            if bo is not None:
                pool.tensor_tensor(k.x[:], k.x[:], bo[:].unsqueeze(1).to_broadcast([P, TILES, DM]), ALU.add)

        @block.tensor
        def _(pe):
            pe.sem_inc(v_mm, 1)
            with pe.Fori(0, NCH) as i:
                for n, w in enumerate((wq, wk)):
                    pe.wait_ge(lo_done, i * 2 + n + 1)
                    pe.matmul(k.ps[:, n, :], w[:], xT[:, sl(i * CHUNK, CHUNK)], start=True,
                              stop=True).then_inc(qk_mm, 1)
                pe.wait_ge(v_done, i + 1)
                pe.wait_ge(x_copied, i + 1)
                for t in range(TPC):
                    ins = pe.matmul(k.ps[:, 2, t * P:t * P + P], xc[:, t * P:t * P + P], wv[:], start=True, stop=True)
                ins.then_inc(v_mm, 1)

        @block.scalar
        def _(act):
            with act.Fori(0, NCH) as i:
                for n in range(2):
                    act.wait_ge(qk_mm, i * 2 + n + 1)
                    act.wait_ge(stored, i * 96 + 96)
                    act.activation(hi[:, n, :], k.ps[:, n, :], ACT.Copy).then_inc(hi_done, 1)

        @block.vector
        def _(dve):
            dve.sem_inc(lo_done, 2)
            dve.sem_inc(v_done, 1)
            with dve.Fori(0, NCH) as i:
                for n in range(2):
                    dve.wait_ge(hi_done, i * 2 + n + 1)
                    dve.wait_ge(stored, i * 96 + 96)
                    dve.tensor_tensor(lo[:, n, :], k.ps[:, n, :], hi[:, n, :], ALU.subtract).then_inc(lo_done, 1)
                dve.wait_ge(v_mm, i + 2)
                dve.tensor_copy(k.v[:, sl(i * TPC, TPC), :], k.ps[:, 2, :].rearrange("p (t c) -> p t c", c=P)
                                ).then_inc(v_done, 1)

        @block.sync
        def _(sp):
            sp.sem_inc(stored, 96)
            sp.wait_ge(const_set, 2)
            zeros = const[:, 0, :].unsqueeze(1).to_broadcast([P, BATCH, SEQ])
            for dst in (k.qs, k.ks):
                sp.dma_start(dst[:, :, 3, :].rearrange("b c t -> c b t"), zeros).then_inc(const_stored, 16)
            sp.wait_ge(const_stored, 32)
            ones = const[0:HEADS, 1, :].unsqueeze(1).to_broadcast([HEADS, BATCH, SEQ])
            sp.dma_start(k.ks[:, 0:P:HD, 3, :].rearrange("b c t -> c b t"), ones).then_inc(const_stored, 16)
            with sp.Fori(0, NCH) as i:
                sp.wait_ge(lo_done, i * 2 + 4)
                for dst, n, parts in ((k.qs, 0, (hi, hi, lo)), (k.ks, 1, (hi, lo, hi))):
                    for r, part in enumerate(parts):
                        sp.dma_start(dst[sl(i * 2, 2), :, r, :].rearrange("b c t -> c b t"),
                                     part[:, n, :].rearrange("p (b t) -> p b t", b=2)).then_inc(stored, 16)
            sp.wait_ge(stored, NCH * 96 + 96)
            sp.wait_ge(const_stored, 48)


def attend(k, tag, wo):
    nc = k.nc
    scale = 1.0 / float(HD) ** 0.5
    BLK = [(0, 0), (1, 0), (1, 1)]
    s_mm, s_free, t_mm, p_ready = k.sem(f"{tag}_s"), k.sem(f"{tag}_sf"), k.sem(f"{tag}_t"), k.sem(f"{tag}_p")
    pv_mm, cx_ready, neg_ready, mt_mm = k.sem(f"{tag}_pv"), k.sem(f"{tag}_cx"), k.sem(f"{tag}_ng"), k.sem(f"{tag}_mt")
    m_copied, m_stored = k.sem(f"{tag}_mc"), k.sem(f"{tag}_ms")
    s_in = [k.sem(f"{tag}_sin{m}") for m in range(2)]
    t_in = [k.sem(f"{tag}_tin{m}") for m in range(2)]
    v_set, v_copied, blk_set = k.sem(f"{tag}_vs"), k.sem(f"{tag}_vc"), k.sem(f"{tag}_bs")
    ct_mm, den_done, norm_done, back_mm = k.sem(f"{tag}_ct"), k.sem(f"{tag}_dn"), k.sem(f"{tag}_nd"), k.sem(f"{tag}_bk")
    back_copied, o_mm, x_added = k.sem(f"{tag}_bc"), k.sem(f"{tag}_o"), k.sem(f"{tag}_xa")
    S_B, T_B, PV_B, CT_B, MISC_B = (0, 1), (2, 3), (4, 5), 6, 7
    with ExitStack() as st, nc.Block() as block:
        qst = [k.sb(f"{tag}_qst{m}", [P, NG, SEQ], F16, ctx=st) for m in range(2)]
        kst = [k.sb(f"{tag}_kst{m}", [P, NG, SEQ], F16, ctx=st) for m in range(2)]
        qbl = [k.sb(f"{tag}_qbl{m}", [P, NG, 4, SEQ], F16, ctx=st) for m in range(2)]
        kbl = [k.sb(f"{tag}_kbl{m}", [P, NG, 4, SEQ], F16, ctx=st) for m in range(2)]
        va = [k.sb(f"{tag}_va{m}", [P, 2, HEADS, 32], ctx=st) for m in range(2)]
        p0 = k.sb(f"{tag}_p0", [P, NG, 4, SEQ], ctx=st)
        p1 = k.sb(f"{tag}_p1", [P, NG, 4, P], ctx=st)
        mx = k.sb(f"{tag}_mx", [P, 3, HEADS], ctx=st)
        neg = k.sb(f"{tag}_neg", [P, 2, HEADS], ctx=st)
        mT = k.sb(f"{tag}_mT", [HEADS, SEQ], F16, ctx=st)
        cx = k.sb(f"{tag}_cx_sb", [P, 2, NG, SEQ], ctx=st)
        rden = k.sb(f"{tag}_rden", [P, 2, HEADS], ctx=st)
        cn = k.sb(f"{tag}_cn", [P, 2, DM], ctx=st)
        cT = k.sb(f"{tag}_cT", [P, SEQ], ctx=st)

        def b_of(batch):
            return batch[0] * 2 + batch[1]

        def steps(engine, step):
            def of(s):
                return (s // 2, s % 2) if 0 <= s < BATCH else None

            for s in range(4):
                step(of(s), of(s - 1), of(s - 2), of(s - 3))
            with engine.Fori(0, BATCH // 2 - 2) as j:
                step((j + 2, 0), (j + 1, 1), (j + 1, 0), (j, 1))
                step((j + 2, 1), (j + 2, 0), (j + 1, 1), (j + 1, 0))
            for s in range(BATCH, BATCH + 3):
                step(None, of(s - 1), of(s - 2), of(s - 3))

        @block.sync
        def _(sp):
            def load_scores(batch):
                b, m = b_of(batch), batch[1]
                src = k.qs[sl(b, 1)].rearrange("b (g c) r t -> (b c r) g t", g=NG)
                k_src = k.ks[sl(b, 1)].rearrange("b (g c) r t -> (b c r) g t", g=NG)
                sp.wait_ge(s_mm, b * 12 + 1)
                sp.dma_start(qst[m][:], src).then_inc(s_in[m], 16)
                for q in range(4):
                    sp.dma_start(kbl[m][32 * q:32 * q + 32, :, q, :], k_src[32 * q:32 * q + 32]).then_inc(s_in[m], 16)

            def load_k(batch):
                b, m = b_of(batch), batch[1]
                sp.wait_ge(t_mm, b * 12 + 1)
                src = k.ks[sl(b, 1)].rearrange("b (g c) r t -> (b c r) g t", g=NG)
                sp.dma_start(kst[m][:], src).then_inc(t_in[m], 16)

            def load_q(batch):
                b, m = b_of(batch), batch[1]
                src = k.qs[sl(b, 1)].rearrange("b (g c) r t -> (b c r) g t", g=NG)
                sp.wait_ge(m_stored, b * 16 + 16)
                for q in range(4):
                    sp.dma_start(qbl[m][32 * q:32 * q + 32, :, q, :], src[32 * q:32 * q + 32]).then_inc(t_in[m], 16)

            def step(new, mid, old, done):
                if new is not None and not (isinstance(new[0], int) and new == (0, 0)):
                    load_scores(new)
                if mid is not None:
                    b = b_of(mid)
                    load_k(mid)
                    sp.wait_ge(m_copied, b + 1)
                    sp.dma_start(k.qs[sl(b, 1), 0:P:HD, 3, :].rearrange("b c t -> (b c) t"),
                                 mT[:]).then_inc(m_stored, 16)
                    load_q(mid)

            sp.wait_ge(blk_set, 4)
            load_scores((0, 0))
            steps(sp, step)

        @block.gpsimd
        def _(pool):
            for m in range(2):
                pool.memset(qbl[m][:], 0.0).then_inc(blk_set, 1)
                pool.memset(kbl[m][:], 0.0).then_inc(blk_set, 1)
            for m in range(2):
                pool.memset(va[m][:], 0.0).then_inc(v_set, 1)
            pool.wait_ge(v_set, 2)
            for m in range(2):
                pool.memset(va[m][:, :, :, HD:HD + 1], 1.0).then_inc(v_set, 1)
            pool.wait_ge(v_set, 4)

            def copy_v(batch):
                b = b_of(batch)
                pool.wait_ge(pv_mm, b * NG + 1)
                pool.tensor_copy(va[batch[1]][:, :, :, 0:HD],
                                 k.v[:, sl(b * 2, 2), :].rearrange("p t (h d) -> p t h d", d=HD)
                                 ).then_inc(v_copied, 1)

            def step(new, mid, old, done):
                if old is not None:
                    copy_v(old)

            steps(pool, step)

        @block.tensor
        def _(pe):
            pe.sem_inc(s_mm, 13)
            pe.sem_inc(t_mm, 13)
            pe.sem_inc(pv_mm, NG + 1)
            pe.sem_inc(mt_mm, 1)
            pe.sem_inc(back_mm, 1)
            pe.sem_inc(o_mm, 1)
            pe.sem_inc(ct_mm, 3)
            pe.wait_ge(v_set, 4)

            def scores(batch, g, block):
                h, m = batch
                qt, kt = BLK[block]
                n = g * 3 + block
                pe.wait_ge(s_free, b_of(batch) * 12 + n + 1)
                o = k.ps[:, S_B[n % 2], :]
                ins = pe.matmul(o, qst[m][:, g, qt * P:qt * P + P], kbl[m][:, g, :, kt * P:kt * P + P],
                                start=True, stop=(qt != kt))
                if qt == kt:
                    ins = pe.matmul(o, k.ident16[:], k.mask_qk[:], start=False, stop=True)
                ins.then_inc(s_mm, 1)

            def scores_T(batch, g, block):
                h, m = batch
                qt, kt = BLK[block]
                n = g * 3 + block
                pe.wait_ge(p_ready, b_of(batch) * 12 + n + 1)
                o = k.ps[:, T_B[n % 2], :]
                ins = pe.matmul(o, kst[m][:, g, kt * P:kt * P + P], qbl[m][:, g, :, qt * P:qt * P + P],
                                start=True, stop=(qt != kt))
                if qt == kt:
                    ins = pe.matmul(o, k.ident16[:], k.mask_kq[:], start=False, stop=True)
                ins.then_inc(t_mm, 1)

            def values(batch, g):
                h, m = batch
                pe.wait_ge(p_ready, 2 + b_of(batch) * 12 + g * 3 + 3)
                pe.wait_ge(cx_ready, b_of(batch) * NG + g + 1)
                for j in range(4):
                    o = k.ps[32 * j:32 * j + 32, PV_B[g % 2], 0:SEQ]
                    pe.matmul(o, va[m][:, 0, 4 * g + j, :], p0[:, g, j, :], start=True, stop=False)
                    ins = pe.matmul(o[:, P:SEQ], va[m][:, 1, 4 * g + j, :], p1[:, g, j, :], start=False, stop=True)
                ins.then_inc(pv_mm, 1)

            def turn_max(batch, alone):
                b = b_of(batch)
                pe.wait_ge(neg_ready, b + 1)
                if not alone:
                    pe.wait_ge(back_copied, b - 1)
                for qt in range(2):
                    ins = pe.transpose(k.ps[0:HEADS, MISC_B, qt * P:qt * P + P], neg[:, qt, :], k.ident[:])
                ins.then_inc(mt_mm, 1)

            def turn_values(batch, qt):
                b = b_of(batch)
                pe.wait_ge(cx_ready, 2 + b * NG + 4)
                if qt == 0:
                    pe.wait_ge(x_added, b + 1)
                else:
                    pe.wait_ge(norm_done, b * 2 + 1)
                for g in range(NG):
                    ins = pe.transpose(k.ps[:, CT_B, g * P:g * P + P], cx[:, batch[1], g, qt * P:qt * P + P], k.ident[:])
                ins.then_inc(ct_mm, 1)

            def turn_back(batch, max_copied):
                b = b_of(batch)
                if max_copied:
                    pe.wait_ge(m_copied, b + 3)
                for qt in range(2):
                    pe.wait_ge(norm_done, b * 2 + qt + 1)
                    ins = pe.transpose(k.ps[:, MISC_B, SEQ + qt * P:SEQ + qt * P + P], cn[:, qt, :], k.ident[:])
                ins.then_inc(back_mm, 1)

            def output(batch):
                b = b_of(batch)
                pe.wait_ge(back_copied, b + 2)
                for qt in range(2):
                    ins = pe.matmul(k.ps[:, CT_B, qt * P:qt * P + P], cT[:, qt * P:qt * P + P], wo[:],
                                    start=True, stop=True)
                ins.then_inc(o_mm, 1)

            def step(new, mid, old, done):
                for g in range(NG):
                    if g == 0 and new is not None:
                        pe.wait_ge(s_in[new[1]], new[0] * 80 + 80)
                    if g == 0 and old is not None:
                        pe.wait_ge(t_in[old[1]], old[0] * 80 + 80)
                        pe.wait_ge(v_copied, b_of(old) + 1)
                    for block in range(2):
                        if new is not None:
                            scores(new, g, block)
                        if old is not None:
                            scores_T(old, g, block)
                    if mid is not None and g == 0:
                        turn_max(mid, mid in ((0, 0), (0, 1), (1, 0)) if isinstance(mid[0], int) else False)
                    if done is not None:
                        if g == 0:
                            values(done, NG - 1)
                        elif g < 3:
                            turn_values(done, g - 1)
                        else:
                            turn_back(done, mid is not None)
                    if new is not None:
                        scores(new, g, 2)
                    if old is not None:
                        if g:
                            values(old, g - 1)
                        scores_T(old, g, 2)
                if done is not None:
                    output(done)

            steps(pe, step)

        @block.scalar
        def _(act):
            act.sem_inc(p_ready, 2)
            act.sem_inc(back_copied, 1)

            def step(new, mid, old, done):
                if mid is not None:
                    b = b_of(mid)
                    act.wait_ge(mt_mm, b + 2)
                    if not (isinstance(b, int) and b == 0):
                        act.wait_ge(m_stored, b * 16)
                    act.activation(mT[:], k.ps[0:HEADS, MISC_B, 0:SEQ], ACT.Copy).then_inc(m_copied, 1)
                for g in range(NG):
                    if done is not None and g == 3:
                        b = b_of(done)
                        act.wait_ge(back_mm, b + 2)
                        act.wait_ge(o_mm, b + 1)
                        act.activation(cT[:], k.ps[:, MISC_B, SEQ:2 * SEQ], ACT.Copy).then_inc(back_copied, 1)
                    if old is not None:
                        b = b_of(old)
                        for n, (qt, kt) in enumerate(BLK):
                            act.wait_ge(t_mm, 13 + b * 12 + g * 3 + n + 1)
                            if n == 0:
                                act.wait_ge(pv_mm, b * NG + g + 2)
                            dst = p0[:, g, :, qt * P:qt * P + P] if kt == 0 else p1[:, g, :, :]
                            act.activation(dst, k.ps[:, T_B[(g * 3 + n) % 2], :].rearrange("p (j q) -> p j q", j=4),
                                           ACT.Exp, scale=scale).then_inc(p_ready, 1)

            steps(act, step)

        @block.vector
        def _(dve):
            dve.sem_inc(s_free, 2)
            dve.sem_inc(cx_ready, 2)
            dve.sem_inc(x_added, 1)

            def maxima(batch, g):
                b = b_of(batch)
                if g == 0 and not (isinstance(b, int) and b == 0):
                    dve.wait_ge(neg_ready, b)
                for n, (qt, kt) in enumerate(BLK):
                    dve.wait_ge(s_mm, 13 + b * 12 + g * 3 + n + 1)
                    dve.tensor_reduce(mx[:, n, g * 4:g * 4 + 4],
                                      k.ps[:, S_B[(g * 3 + n) % 2], :].rearrange("p (j q) -> p j q", j=4),
                                      AX.X, ALU.max, negate=True).then_inc(s_free, 1)

            def copy_values(batch, g):
                b = b_of(batch)
                dve.wait_ge(pv_mm, NG + 1 + b * NG + g + 1)
                if g == 0:
                    dve.wait_ge(ct_mm, b * 2 + 1)
                dve.tensor_copy(cx[:, batch[1], g, :], k.ps[:, PV_B[g % 2], 0:SEQ]).then_inc(cx_ready, 1)

            def normalize(batch, qt):
                b = b_of(batch)
                dve.wait_ge(ct_mm, 3 + b * 2 + qt + 1)
                ct = k.ps[:, CT_B, :].rearrange("p (h r) -> p h r", r=32)
                dve.reciprocal(rden[:, qt, :], ct[:, :, HD]).then_inc(den_done, 1)
                dve.wait_ge(den_done, b * 2 + qt + 1)
                if qt == 0:
                    dve.wait_ge(back_mm, b + 1)
                dve.tensor_tensor(cn[:, qt, :].rearrange("p (h d) -> p h d", d=HD), ct[:, :, 0:HD],
                                  rden[:, qt, :].unsqueeze(2).to_broadcast([P, HEADS, HD]),
                                  ALU.mult).then_inc(norm_done, 1)

            def step(new, mid, old, done):
                for g in range(NG):
                    if new is not None:
                        maxima(new, g)
                    if done is not None:
                        if g == 0:
                            copy_values(done, NG - 1)
                        elif g < 3:
                            normalize(done, g - 1)
                    if g == 3 and new is not None:
                        b = b_of(new)
                        dve.wait_ge(s_free, 2 + b * 12 + 12)
                        dve.wait_ge(mt_mm, b + 1)
                        dve.tensor_copy(neg[:, 0, :], mx[:, 0, :])
                        dve.tensor_tensor(neg[:, 1, :], mx[:, 1, :], mx[:, 2, :], ALU.min).then_inc(neg_ready, 1)
                    if old is not None and g > 0:
                        copy_values(old, g - 1)
                if done is not None:
                    b = b_of(done)
                    dve.wait_ge(o_mm, b + 2)
                    xs = k.x[:, sl(b * 2, 2), :]
                    dve.tensor_tensor(xs, xs, k.ps[:, CT_B, 0:SEQ].rearrange("p (t c) -> p t c", c=P),
                                      ALU.add).then_inc(x_added, 1)

            steps(dve, step)



HID1 = 384
KT1 = HID1 // P


def ffn1(k):
    nc, w = k.nc, k.w
    dequant = k.sem("f1_dequant")
    gate_mm, up_mm, sg_ready, h_ready = k.sem("f1_gate"), k.sem("f1_up"), k.sem("f1_silu"), k.sem("f1_h")
    down_mm, added = k.sem("f1_down"), k.sem("f1_add")
    with ExitStack() as st, nc.Block() as block:
        sg = k.sb("f1_sg", [P, KT1, CHUNK], ctx=st)
        h = k.sb("f1_h_sb", [P, 2, KT1, CHUNK], ctx=st)
        wg, wu = k.sb("f1_wg", [P, HID1], ctx=st), k.sb("f1_wu", [P, HID1], ctx=st)
        wd = k.sb("f1_wd", [P, KT1, DM], ctx=st)

        def passes(engine, gated, down):
            gated((0, 0))
            with engine.Fori(0, NCH // 2 - 1) as j:
                gated((j, 1))
                down((j, 0))
                gated((j + 1, 0))
                down((j, 1))
            gated((NCH // 2 - 1, 1))
            down((NCH // 2 - 1, 0))
            down((NCH // 2 - 1, 1))

        @block.gpsimd
        def _(pool):
            for a, b in ((wg, w["f1_gate"]), (wu, w["f1_up"]), (wd, w["f1_down"])):
                pool.tensor_scalar(a[:], b[:], 1.0 / 127.0, None, ALU.mult).then_inc(dequant, 1)

        @block.tensor
        def _(pe):
            pe.wait_ge(dequant, 3)

            def gated(c):
                i = c[0] * 2 + c[1]
                xc = k.xT[:, sl(i * CHUNK, CHUNK)]
                for t in range(KT1):
                    pe.wait_ge(h_ready, i * KT1 + t + 1)
                    pe.matmul(k.ps[:, t, :], wg[:, t * P:t * P + P], xc, start=True, stop=True).then_inc(gate_mm, 1)
                    pe.matmul(k.ps[:, KT1 + t, :], wu[:, t * P:t * P + P], xc, start=True,
                              stop=True).then_inc(up_mm, 1)

            def down(c):
                i = c[0] * 2 + c[1]
                pe.wait_ge(h_ready, KT1 + i * KT1 + KT1)
                pe.wait_ge(added, i + 1)
                for t in range(TPC):
                    for kt in range(KT1):
                        ins = pe.matmul(k.ps[:, 6 + c[1], t * P:t * P + P], h[:, c[1], kt, t * P:t * P + P], wd[:, kt, :],
                                        start=(kt == 0), stop=(kt == KT1 - 1))
                ins.then_inc(down_mm, 1)

            passes(pe, gated, down)

        @block.scalar
        def _(act):
            def gated(c):
                i = c[0] * 2 + c[1]
                for t in range(KT1):
                    act.wait_ge(gate_mm, i * KT1 + t + 1)
                    act.wait_ge(h_ready, i * KT1 + t + 1)
                    act.activation(sg[:, t, :], k.ps[:, t, :], ACT.Silu).then_inc(sg_ready, 1)

            passes(act, gated, lambda c: None)

        @block.vector
        def _(dve):
            dve.sem_inc(h_ready, KT1)
            dve.sem_inc(added, 2)

            def gated(c):
                i = c[0] * 2 + c[1]
                dve.wait_ge(added, i + 1)
                for t in range(KT1):
                    dve.wait_ge(sg_ready, i * KT1 + t + 1)
                    dve.wait_ge(up_mm, i * KT1 + t + 1)
                    dve.tensor_tensor(h[:, c[1], t, :], sg[:, t, :], k.ps[:, KT1 + t, :], ALU.mult).then_inc(h_ready, 1)

            def down(c):
                i = c[0] * 2 + c[1]
                dve.wait_ge(down_mm, i + 1)
                xs = k.x[:, sl(i * TPC, TPC), :]
                dve.tensor_tensor(xs, xs, k.ps[:, 6 + c[1], :].rearrange("p (t c) -> p t c", c=P),
                                  ALU.add).then_inc(added, 1)

            passes(dve, gated, down)



HID2 = 512
KT2 = HID2 // P
WIN = 3


def layer2_body(k):
    nc, w = k.nc, k.w
    prep = k.sem("l2_prep")
    q_mm, copied, pj_ready, s_mm = k.sem("w_qkv"), k.sem("w_copied"), k.sem("w_pj"), k.sem("w_s")
    m_cp, mx_step, d_ready, e_ready = k.sem("w_m"), k.sem("w_mx"), k.sem("w_d"), k.sem("w_e")
    tail_step, y_ready = k.sem("w_tail"), k.sem("w_y")
    a_mm, sg_ready, h_ready = k.sem("f2_a"), k.sem("f2_sg"), k.sem("f2_h")
    b_mm, g1_done, c_mm, g2_done = k.sem("f2_b"), k.sem("f2_g1"), k.sem("f2_c"), k.sem("f2_g2")
    d_mm, x_added = k.sem("f2_d"), k.sem("f2_x")
    OUT_B, W_B = 4, (5, 6, 7)
    scale = 1.0 / float(HD) ** 0.5
    MXS, TLS = 2, 10
    with ExitStack() as st, nc.Block() as block:
        h1 = k.sb("f2_h1", [P, KT2, CHUNK], ctx=st)
        h2 = k.sb("f2_h2", [P, KT2, CHUNK], ctx=st)
        h3 = k.sb("f2_h3", [P, KT2, CHUNK], ctx=st)
        sg = k.sb("f2_sg_sb", [P, 2, CHUNK], ctx=st)
        q = k.sb("w_q_sb", [P, 2, SEQ], ctx=st)
        kk = k.sb("w_k_sb", [P, 2, WIN - 1 + SEQ], ctx=st)
        v = k.sb("w_v_sb", [P, 2, WIN - 1 + SEQ], ctx=st)
        pj = k.sb("w_pj_sb", [P, WIN, 2, SEQ], ctx=st)
        mx = k.sb("w_mx_sb", [P, 2, SEQ], ctx=st)
        e = k.sb("w_e_sb", [P, WIN, 2, SEQ], ctx=st)
        den = k.sb("w_den", [P, 2, SEQ], ctx=st)
        rden = k.sb("w_rden", [P, 2, SEQ], ctx=st)
        y = k.sb("w_y_sb", [P, CHUNK], ctx=st)

        def bank(n):
            return k.ps[:, n, :].rearrange("p (b t) -> p b t", b=2)

        def shifted(a, j):
            return a[:, :, WIN - 1 - j:WIN - 1 - j + SEQ]

        @block.gpsimd
        def _(pool):
            pool.memset(kk[:], 0.0).then_inc(prep, 1)
            pool.memset(v[:], 0.0).then_inc(prep, 1)
            pool.tensor_tensor(w["w3"][:], w["w3"][:], w["s3"][:].unsqueeze(1).to_broadcast([P, KT2, DM]),
                               ALU.mult).then_inc(prep, 1)
            pool.tensor_tensor(k.x[:], k.x[:], w["a2bo"][:].unsqueeze(1).to_broadcast([P, TILES, DM]),
                               ALU.add).then_inc(prep, 1)

        @block.tensor
        def _(pe):
            pe.sem_inc(s_mm, 3)
            pe.sem_inc(b_mm, 4)
            pe.sem_inc(c_mm, 4)
            pe.sem_inc(d_mm, 1)
            pe.wait_ge(prep, 4)
            with pe.Fori(0, NCH) as i:
                xc = k.xT[:, sl(i * CHUNK, CHUNK)]
                pe.wait_ge(d_ready, i + 1)
                for n, name in enumerate(("a2q", "a2k", "a2v")):
                    pe.matmul(k.ps[:, W_B[n], :], w[name][:], xc, start=True, stop=True).then_inc(q_mm, 1)
                for t in range(KT2):
                    if t == 0:
                        pe.wait_ge(g2_done, i * 4 + 4)
                    if t > 1:
                        pe.wait_ge(h_ready, 2 + i * 4 + t - 1)
                    pe.matmul(k.ps[:, t % 2, :], w["w1"][:, t * P:t * P + P], xc, start=True, stop=True).then_inc(a_mm, 1)
                    pe.matmul(k.ps[:, 2 + t % 2, :], w["w2"][:, t * P:t * P + P], xc, start=True,
                              stop=True).then_inc(a_mm, 1)
                for j in range(WIN):
                    pe.wait_ge(copied, i * 3 + 3)
                    pe.wait_ge(pj_ready, 3 + i * 3 + j + 1)
                    pe.matmul(k.ps[:, W_B[j], :], w["heads"][:], pj[:, j].rearrange("p b t -> p (b t)"),
                              start=True, stop=True).then_inc(s_mm, 1)
                for t in range(KT2):
                    for kt in range(KT2):
                        if t == 0:
                            pe.wait_ge(h_ready, 2 + i * 4 + max(3, kt + 1))
                        ins = pe.matmul(k.ps[:, t, :], w["h1"][:, kt, t * P:t * P + P], h1[:, kt, :],
                                        start=(kt == 0), stop=(kt == KT2 - 1))
                    ins.then_inc(b_mm, 1)
                for t in range(KT2):
                    for kt in range(KT2):
                        if t == 0 or kt == 0:
                            pe.wait_ge(g1_done, i * 4 + max(t, kt) + 1)
                        ins = pe.matmul(k.ps[:, t, :], w["h2"][:, kt, t * P:t * P + P], h2[:, kt, :],
                                        start=(kt == 0), stop=(kt == KT2 - 1))
                    ins.then_inc(c_mm, 1)
                pe.wait_ge(x_added, i + 1)
                pe.wait_ge(y_ready, 1 + i + 1)
                for t in range(TPC):
                    pe.matmul(k.ps[:, OUT_B, t * P:t * P + P], y[:, t * P:t * P + P], w["a2o"][:],
                              start=(t == 0), stop=False, skip_group_check=True)
                for kt in range(KT2):
                    pe.wait_ge(g2_done, 4 + i * 4 + kt + 1)
                    for t in range(TPC):
                        ins = pe.matmul(k.ps[:, OUT_B, t * P:t * P + P], h3[:, kt, t * P:t * P + P], w["w3"][:, kt, :],
                                        start=False, stop=(kt == KT2 - 1), skip_group_check=True)
                ins.then_inc(d_mm, 1)

        @block.scalar
        def _(act):
            act.sem_inc(g2_done, 4)
            act.wait_ge(prep, 2)
            with act.Fori(0, NCH) as i:
                for n, (dst, b) in enumerate(((q[:], "a2bq"), (kk[:, :, 2:], "a2bk"), (v[:, :, 2:], "a2bv"))):
                    act.wait_ge(q_mm, i * 3 + n + 1)
                    if n == 0:
                        act.wait_ge(pj_ready, i * 3 + 3)
                    if n == 2:
                        act.wait_ge(y_ready, i + 1)
                    act.activation(dst, bank(W_B[n]), ACT.Identity, bias=w[b][:, 0:1]).then_inc(copied, 1)
                for t in range(KT2):
                    act.wait_ge(a_mm, i * 8 + 2 * t + 1)
                    act.wait_ge(h_ready, i * 4 + t + 1)
                    act.activation(sg[:, t % 2, :], k.ps[:, t % 2, :], ACT.Silu,
                                   scale=w["s1"][:, t:t + 1]).then_inc(sg_ready, 1)
                act.wait_ge(s_mm, 3 + i * 3 + 1)
                act.wait_ge(d_ready, i + 1)
                act.activation(mx[:], bank(W_B[0]), ACT.Copy).then_inc(m_cp, 1)
                for t in range(KT2):
                    act.wait_ge(b_mm, 4 + i * 4 + t + 1)
                    act.wait_ge(c_mm, i * 4 + 4)
                    act.activation(h2[:, t, :], k.ps[:, t, :], ACT.Gelu, scale=w["hs1"][:, t:t + 1]).then_inc(g1_done, 1)
                act.wait_ge(d_ready, 1 + i + 1)
                act.activation(e[:], e[:], ACT.Exp, scale=scale).then_inc(e_ready, 1)
                for t in range(KT2):
                    act.wait_ge(c_mm, 4 + i * 4 + t + 1)
                    act.wait_ge(d_mm, i + 1)
                    act.activation(h3[:, t, :], k.ps[:, t, :], ACT.Gelu, scale=w["hs2"][:, t:t + 1]).then_inc(g2_done, 1)

        @block.vector
        def _(dve):
            dve.sem_inc(pj_ready, 3)
            dve.sem_inc(h_ready, 2)
            dve.sem_inc(d_ready, 1)
            dve.sem_inc(y_ready, 1)
            dve.sem_inc(x_added, 1)
            dve.wait_ge(prep, 4)
            with dve.Fori(0, NCH) as i:
                n = 0

                def link(ins):
                    nonlocal n
                    n += 1
                    ins.then_inc(tail_step, 1)
                    dve.wait_ge(tail_step, i * TLS + n)

                dve.wait_ge(copied, i * 3 + 2)
                dve.wait_ge(s_mm, i * 3 + 3)
                for j in range(WIN):
                    dve.tensor_tensor(pj[:, j], q[:], shifted(kk, j), ALU.mult).then_inc(pj_ready, 1)
                dve.wait_ge(b_mm, i * 4 + 4)
                for t in range(KT2):
                    dve.wait_ge(sg_ready, i * 4 + t + 1)
                    dve.wait_ge(a_mm, i * 8 + 2 * t + 2)
                    dve.scalar_tensor_tensor(out=h1[:, t, :], in0=k.ps[:, 2 + t % 2, :], scalar=w["s2"][:, t:t + 1],
                                             in1=sg[:, t % 2, :], op0=ALU.mult, op1=ALU.mult).then_inc(h_ready, 1)
                dve.wait_ge(m_cp, i + 1)
                dve.wait_ge(s_mm, 3 + i * 3 + 3)
                for j in (1, 2):
                    dve.tensor_tensor(mx[:, :, j:], mx[:, :, j:], bank(W_B[j])[:, :, j:], ALU.max).then_inc(mx_step, 1)
                    dve.wait_ge(mx_step, i * MXS + j)
                for j in range(WIN):
                    ins = dve.tensor_tensor(e[:, j], bank(W_B[j]), mx[:], ALU.subtract)
                ins.then_inc(d_ready, 1)
                dve.wait_ge(e_ready, i + 1)
                dve.memset(e[:, 1, :, 0:1], 0.0)
                link(dve.memset(e[:, 2, :, 0:2], 0.0))
                link(dve.tensor_tensor(den[:], e[:, 0], e[:, 1], ALU.add))
                link(dve.tensor_tensor(den[:], den[:], e[:, 2], ALU.add))
                link(dve.reciprocal(rden[:], den[:]))
                for j in range(WIN):
                    link(dve.tensor_tensor(e[:, j], e[:, j], shifted(v, j), ALU.mult))
                link(dve.tensor_tensor(e[:, 0], e[:, 0], e[:, 1], ALU.add))
                link(dve.tensor_tensor(e[:, 0], e[:, 0], e[:, 2], ALU.add))
                dve.wait_ge(d_mm, i + 1)
                link(dve.tensor_tensor(den[:], e[:, 0], rden[:], ALU.mult))
                dve.tensor_copy(y[:].rearrange("p (b t) -> p b t", b=2), den[:]).then_inc(y_ready, 1)
                assert n == TLS
                dve.wait_ge(d_mm, 1 + i + 1)
                xs = k.x[:, sl(i * TPC, TPC), :]
                dve.tensor_tensor(xs, xs, k.ps[:, OUT_B, :].rearrange("p (t c) -> p t c", c=P),
                                  ALU.add).then_inc(x_added, 1)


def layer2_weights(k, c, weight, everywhere, column):
    d = k.dram
    for n in "qkvo":
        weight(c, "a2" + n, [P, DM], d[f"a2{n}T"])
    for n in "qkv":
        column(c, "a2b" + n, d["L2_attn_b" + n])
    everywhere(c, "a2bo", d["L2_attn_bo"])
    everywhere(c, "s3", d["L2_ffn_w3_s"])
    weight(c, "heads", [P, P], d["head_blocks"])
    for n in ("w1", "w2"):
        weight(c, n, [P, HID2], d[f"f2_{n}T"])
    for n, s in (("s1", "w1_s"), ("s2", "w2_s"), ("hs1", "h1_s"), ("hs2", "h2_s")):
        weight(c, n, [P, KT2], d[f"f2_{s}"])
    for n in ("h1", "h2"):
        weight(c, n, [P, KT2, HID2], d[f"f2_{n}T"].rearrange("(t p) o -> p t o", p=P))
    weight(c, "w3", [P, KT2, DM], d["f2_w3T"].rearrange("(t p) o -> p t o", p=P))


def layer2(k):
    loads_arrived(k, 2)
    norm(k, "n2", k.x, k.xT)
    layer2_body(k)



CYCLES = 3


def global_net(k, beta):
    nc, w = k.nc, k.w
    v, a, m = k.sem("g_dve"), k.sem("g_act"), k.sem("g_pe")
    with ExitStack() as st, nc.Block() as block:
        mean = k.sb("g_mean", [P, BATCH], ctx=st)
        g1, g2 = k.sb("g_h1", [P, BATCH], ctx=st), k.sb("g_h2", [P, BATCH], ctx=st)
        t3 = k.sb("g_t", [P, BATCH], ctx=st)

        @block.vector
        def _(dve):
            dve.tensor_reduce(mean[:], k.xT[:].rearrange("p (b t) -> p b t", b=BATCH), AX.X, ALU.add).then_inc(v, 1)
            dve.wait_ge(v, 1)
            dve.tensor_scalar(mean[:], mean[:], 1.0 / SEQ, None, ALU.mult).then_inc(v, 1)
            dve.tensor_scalar(k.alpha[:], w["ar"][:], 0.3, None, ALU.mult).then_inc(v, 1)
            dve.tensor_scalar(k.hb4[:], w["cb4"][:], 0.5, None, ALU.mult).then_inc(v, 1)
            dve.tensor_scalar(k.hgb[:], w["gb3"][:], 0.5, None, ALU.mult).then_inc(v, 1)
            dve.wait_ge(a, 3)
            dve.tensor_scalar(beta[:], t3[:], 0.7, None, ALU.mult).then_inc(v, 1)
            dve.wait_ge(v, 6)
            dve.tensor_scalar(beta[:], beta[:], w["ar"][:, 0:1], 0.1, ALU.mult, ALU.add).then_inc(v, 1)

        @block.tensor
        def _(pe):
            pe.wait_ge(v, 2)
            pe.matmul(k.ps[:, 0, 0:BATCH], w["gw1"][:], mean[:], start=True, stop=True).then_inc(m, 1)
            pe.wait_ge(a, 1)
            pe.matmul(k.ps[:, 1, 0:BATCH], w["gw2"][:], g1[:], start=True, stop=True).then_inc(m, 1)
            pe.wait_ge(a, 2)
            pe.matmul(k.ps[:, 2, 0:BATCH], w["gw3"][:], g2[:], start=True, stop=True).then_inc(m, 1)

        @block.scalar
        def _(act):
            act.wait_ge(m, 1)
            act.activation(g1[:], k.ps[:, 0, 0:BATCH], ACT.Gelu, bias=w["gb1"][:, 0:1]).then_inc(a, 1)
            act.wait_ge(m, 2)
            act.activation(g2[:], k.ps[:, 1, 0:BATCH], ACT.Gelu, bias=w["gb2"][:, 0:1]).then_inc(a, 1)
            act.wait_ge(m, 3)
            act.wait_ge(v, 5)
            act.activation(t3[:], k.ps[:, 2, 0:BATCH], ACT.Tanh, bias=k.hgb[:, 0:1], scale=0.5).then_inc(a, 1)


def coupling(k, beta):
    nc, w = k.nc, k.w
    mm = [k.sem(f"c_mm{c}") for c in range(2)]
    fn = [k.sem(f"c_fn{c}") for c in range(2)]
    dv = [k.sem(f"c_dv{c}") for c in range(2)]
    MM, FN, DV = CYCLES * 5 + 1, CYCLES * 4, CYCLES * 4 + 1
    with ExitStack() as st, nc.Block() as block:
        g = [k.sb(f"c_g{c}", [P, 3, CHUNK], ctx=st) for c in range(2)]
        tn = [k.sb(f"c_tanh{c}", [P, 2, SEQ], ctx=st) for c in range(2)]
        tw = [k.sb(f"c_tw{c}", [P, CHUNK], ctx=st) for c in range(2)]
        fin = [k.sb(f"c_fin{c}", [P, CHUNK], ctx=st) for c in range(2)]

        def chunk(i, c):
            return k.xT[:, sl(i * 2 * CHUNK + c * CHUNK, CHUNK)]

        @block.tensor
        def _(pe):
            with pe.Fori(0, NCH // 2) as i:
                for y in range(CYCLES):
                    for layer in range(4):
                        for c in range(2):
                            if layer == 0:
                                pe.wait_ge(dv[c], DV + i * DV + y * 4)
                                pe.matmul(k.ps[:, 4 * c + 3, :], w["twist"][:], chunk(i, c), start=True,
                                          stop=True).then_inc(mm[c], 1)
                                src = chunk(i, c)
                            else:
                                pe.wait_ge(fn[c], i * FN + y * 4 + layer)
                                src = g[c][:, layer - 1, :]
                            pe.matmul(k.ps[:, 4 * c + layer % 3, :], w[f"cw{layer + 1}"][:], src, start=True,
                                      stop=True).then_inc(mm[c], 1)
                for c in range(2):
                    pe.wait_ge(dv[c], DV + i * DV + CYCLES * 4)
                    for t in range(TPC):
                        ins = pe.transpose(k.ps[:, 4 * c + 3, t * P:t * P + P], fin[c][:, t * P:t * P + P], k.ident[:])
                    ins.then_inc(mm[c], 1)

        @block.scalar
        def _(act):
            with act.Fori(0, NCH // 2) as i:
                for y in range(CYCLES):
                    for layer in range(3):
                        for c in range(2):
                            act.wait_ge(mm[c], i * MM + y * 5 + layer + 2)
                            act.activation(g[c][:, layer, :], k.ps[:, 4 * c + layer, :], ACT.Gelu,
                                           bias=w[f"cb{layer + 1}"][:, 0:1]).then_inc(fn[c], 1)
                    for c in range(2):
                        act.wait_ge(mm[c], i * MM + y * 5 + 5)
                        act.wait_ge(dv[c], DV + i * DV + y * 4)
                        act.activation(tn[c][:].rearrange("p b t -> p (b t)"), k.ps[:, 4 * c, :], ACT.Tanh,
                                       bias=k.hb4[:, 0:1], scale=0.5).then_inc(fn[c], 1)

        @block.vector
        def _(dve):
            for c in range(2):
                dve.sem_inc(dv[c], DV)
            with dve.Fori(0, NCH // 2) as i:
                for y in range(CYCLES):
                    for c in range(2):
                        at = i * DV + y * 4 + DV
                        dve.wait_ge(fn[c], i * FN + y * 4 + 4)
                        for b in range(2):
                            dve.tensor_scalar(tn[c][:, b, :], tn[c][:, b, :], k.alpha[:, 0:1],
                                              beta[:, sl(i * 4 + c * 2 + b, 1)], ALU.mult, ALU.add).then_inc(dv[c], 1)
                        dve.wait_ge(dv[c], at + 2)
                        dve.tensor_tensor(tw[c][:], tn[c][:].rearrange("p b t -> p (b t)"), k.ps[:, 4 * c + 3, :],
                                          ALU.mult).then_inc(dv[c], 1)
                        dve.wait_ge(dv[c], at + 3)
                        dst = chunk(i, c) if y < CYCLES - 1 else fin[c][:]
                        dve.tensor_tensor(dst, chunk(i, c), tw[c][:], ALU.add).then_inc(dv[c], 1)
                for c in range(2):
                    dve.wait_ge(mm[c], i * MM + MM)
                    xs = k.x[:, sl(i * 2 * TPC + c * TPC, TPC), :]
                    dve.tensor_tensor(xs, xs, k.ps[:, 4 * c + 3, :].rearrange("p (t c) -> p t c", c=P),
                                      ALU.add).then_inc(dv[c], 1)


def layer3_weights(k, c, weight, column):
    d = k.dram
    for n in "qkvo":
        weight(c, "a3" + n, [P, DM], d[f"a3{n}T"])
    for n in ("cw1", "cw2", "cw3", "cw4", "gw1", "gw2", "gw3"):
        weight(c, n, [P, P], d[n])
    weight(c, "twist", [P, P], d["twist"])
    for n in ("cb1", "cb2", "cb3", "cb4", "gb1", "gb2", "gb3", "ar"):
        column(c, n, d[n])
    k.alpha, k.hb4, k.hgb = k.sb("alpha", [P, 1], ctx=c), k.sb("half_b4", [P, 1], ctx=c), k.sb("half_gb", [P, 1], ctx=c)
    k.beta = k.sb("beta_b", [P, BATCH], ctx=c)


def layer3(k):
    w, beta = k.w, k.beta
    loads_arrived(k, 3)
    norm(k, "n3", k.x, k.xT)
    with ExitStack() as a:
        k.v = k.sb("v_all3", [P, TILES, DM], ctx=a)
        project(k, "pr3", k.xT, w["a3q"], w["a3k"], w["a3v"], None)
        attend(k, "at3", w["a3o"])
    global_net(k, beta)
    coupling(k, beta)


def store(k):
    done = k.sem("out_stored")
    with k.nc.Block() as block:

        @block.sync
        def _(sp):
            sp.dma_start(k.out.rearrange("b (h p) d -> p (b h) d", p=P), k.x[:]).then_inc(done, 16)
            sp.wait_ge(done, 16)


def simple_add(k, tag, dst, src, bias=None):
    done = k.sem(tag)
    with k.nc.Block() as block:

        @block.gpsimd
        def _(pool):
            pool.tensor_tensor(dst[:], dst[:], src[:], ALU.add).then_inc(done, 1)
            if bias is not None:
                pool.wait_ge(done, 1)
                pool.tensor_tensor(dst[:], dst[:], bias[:].unsqueeze(1).to_broadcast([P, TILES, DM]), ALU.add)


UPTO = 99


def loads_arrived(k, layer):
    arrived, loads = k.late[layer]
    with k.nc.Block() as block:

        @block.sync
        def _(sp):
            sp.wait_ge(arrived, 16 * len(loads))


def layer1_weights(k, c, weight, everywhere):
    d = k.dram
    for n in "qkvo":
        weight(c, "a1" + n, [P, DM], d["L1_attn_W" + n])
    everywhere(c, "a1bo", d["L1_attn_bo"])
    weight(c, "f1_gate", [P, HID1], d["f1_gateT"], I32)
    weight(c, "f1_up", [P, HID1], d["f1_upT"], I32)
    weight(c, "f1_down", [P, KT1, DM], d["f1_downT"].rearrange("(t p) c -> p t c", p=P), I32)


def layer1(k):
    loads_arrived(k, 1)
    norm(k, "n1", k.x, k.xT)
    w = k.w
    with ExitStack() as a:
        k.v = k.sb("v_all1", [P, TILES, DM], ctx=a)
        project(k, "pr1", k.xT, w["a1q"], w["a1k"], w["a1v"], w["a1bo"])
        attend(k, "at1", w["a1o"])
    ffn1(k)


def build(nc, dram, out):
    with ExitStack() as ctx:
        k = Program(nc, ctx, dram, out)
        k.ps = ctx.enter_context(nc.psum_tensor("banks", [P, 8, 512], F32))
        k.x = k.sb("x_res", [P, TILES, DM])
        k.xT = k.sb("xnT", [P, BATCH * SEQ])
        k.ident, k.ident16 = k.sb("ident", [P, P]), k.sb("ident16", [P, P], F16)
        k.mirror = k.sb("mirror", [P, P])
        k.mask_kq, k.mask_qk = k.sb("mask_kq", [P, 4, P], F16), k.sb("mask_qk", [P, 4, P], F16)
        k.eps = k.sb("eps", [P, 1])
        k.lag_i, k.lag = k.sb("lag_i", [P, SEQ], I32), k.sb("lag", [P, SEQ])
        k.st, k.mv = k.sb("ln_stats", [P, TILES, 6]), k.sb("ln_mv", [P, TILES, 2])
        k.std, k.rstd, k.z8 = k.sb("ln_std", [P, TILES]), k.sb("ln_rstd", [P, TILES]), k.sb("ln_z", [P, 8, DM])
        k.kpad = nc.dram_tensor("kernel_padded", (DM, P + SEQ), F32).ap()
        k.yT = nc.dram_tensor("conv_out", (DM, BATCH, SEQ), F32).ap()
        k.qs = nc.dram_tensor("q_stacked", (BATCH, P, ROWS, SEQ), F16).ap()
        k.ks = nc.dram_tensor("k_stacked", (BATCH, P, ROWS, SEQ), F16).ap()
        k.w, k.loads = {}, []

        def weight(c, name, shape, src, dt=F32):
            k.w[name] = k.sb("w_" + name, shape, dt, ctx=c)
            k.loads.append((k.w[name][:], src))

        def column(c, name, src):
            weight(c, name, [P, 1], src.rearrange("(p a) -> p a", a=1))

        def everywhere(c, name, src):
            weight(c, name, [P, DM], bass.AP(tensor=src.tensor, offset=src.offset, ap=[[0, P], [1, DM]]))

        k.late = {}
        for layer, declare in ((1, lambda: layer1_weights(k, ctx, weight, everywhere)),
                               (2, lambda: layer2_weights(k, ctx, weight, everywhere, column)),
                               (3, lambda: layer3_weights(k, ctx, weight, column))):
            declare()
            k.late[layer] = (ctx.enter_context(nc.semaphore(f"weights{layer}_arrived")), k.loads)
            k.loads = []
        with ExitStack() as l0:
            column(l0, "ffn_scale", dram["L0_ffn_ln_scale"])
            column(l0, "ffn_bias", dram["L0_ffn_ln_bias"])
            column(l0, "log_dt", dram["L0_attn_log_dt"])
            column(l0, "D", dram["L0_attn_D_param"])
            everywhere(l0, "gamma", dram["L0_attn_ln_gamma"])
            everywhere(l0, "beta", dram["L0_attn_ln_beta"])
            everywhere(l0, "b_out", dram["L0_attn_b_out"])
            weight(l0, "log_A", [P, NST], dram["L0_attn_log_A"])
            weight(l0, "B", [P, NST], dram["L0_attn_B_param"])
            weight(l0, "C", [P, NST], dram["L0_attn_C_param"])
            weight(l0, "gate", [P, NE], dram["gate_wT"])
            weight(l0, "W_out", [P, DM], dram["W_outT"])
            for n in "gu":
                k.w["W" + n] = k.sb("w_W" + n, [P, NE + 1, INTER], ctx=l0)
                k.loads.append((k.w["W" + n][:, 0:NE, :], dram["L0_ffn_W" + n].rearrange("e p i -> p e i")))
                k.loads.append((k.w["W" + n][:, NE, :], dram["L0_ffn_sW" + n]))
            k.w["Wd"] = k.sb("w_Wd", [P, NE + 1, IT, DM], ctx=l0)
            for e in range(NE):
                k.loads.append((k.w["Wd"][:, e], dram["L0_ffn_Wd"][e].rearrange("(t p) d -> p t d", p=P)))
            k.loads.append((k.w["Wd"][:, NE], dram["L0_ffn_sWd"].rearrange("(t p) d -> p t d", p=P)))
            gate_weight = k.sb("gate_weight", [P, TILES, NE], ctx=l0)
            load(k)
            with ExitStack() as mid:
                u = k.sb("ssm_in", [P, 2, DM, BATCH], ctx=mid)
                with ExitStack() as early:
                    z1 = k.sb("xn_tok", [P, TILES, DM], ctx=early)
                    zz = k.sb("zz_tok", [P, TILES, DM], ctx=early)
                    zT = k.sb("zzT", [P, BATCH * SEQ], ctx=early)
                    norm(k, "n0", k.x, k.xT, z1, [late for layer, late in k.late.items() if layer <= UPTO - 1])
                    norm(k, "n0b", z1, zT, zz)
                    simple_add(k, "x_plus_xn", k.x, z1, k.w["b_out"])
                    gates(k, zT, gate_weight)
                    ssm_kernel(k, zz, u)
                convolve(k, u)
            experts(k, k.xT, gate_weight)
        k.end_layer()
        if UPTO >= 2:
            layer1(k)
            k.end_layer()
        if UPTO >= 3:
            layer2(k)
            k.end_layer()
        if UPTO >= 4:
            layer3(k)
        store(k)


_OUTS = [((BATCH, SEQ, DM), "float32")]


TRANSPOSED = {"gate_wT": "L0_ffn_gate_w", "W_outT": "L0_attn_W_out", "f1_gateT": "L1_ffn_w_gate",
              "f1_upT": "L1_ffn_w_up", "f1_downT": "L1_ffn_w_down", "f2_w1T": "L2_ffn_w1_w",
              "f2_w2T": "L2_ffn_w2_w", "f2_h1T": "L2_ffn_h1_w", "f2_h2T": "L2_ffn_h2_w", "f2_w3T": "L2_ffn_w3_w"}
TRANSPOSED |= {f"a{layer}{n}T": f"L{layer}_attn_W{n}" for layer in (2, 3) for n in "qkvo"}


def kernel(**inputs):
    import numpy as np
    import concourse.bacc as bacc
    from concourse.bass_utils import run_bass_kernel_spmd

    nc = bacc.Bacc("TRN2", target_bir_lowering=False, num_devices=1)
    arrays = {n: np.ascontiguousarray(a) for n, a in inputs.items()}
    for new, old in TRANSPOSED.items():
        arrays[new] = np.ascontiguousarray(arrays.pop(old).T)
    for s in ("w1_s", "w2_s", "h1_s", "h2_s"):
        arrays[f"f2_{s}"] = np.ascontiguousarray(arrays.pop(f"L2_ffn_{s}").reshape(-1, P).T)
    for net, n_layers in (("c", 4), ("g", 3)):
        for n in range(1, n_layers + 1):
            a, b = arrays.pop(f"L3_ffn_{net}{'nc'[net == 'g']}_w{n}"), arrays.pop(f"L3_ffn_{net}{'nc'[net == 'g']}_b{n}")
            if n == n_layers:
                a, b = np.repeat(a, P, axis=1), np.repeat(b, P)
            arrays[f"{net}w{n}"] = np.pad(a, ((0, P - a.shape[0]), (0, P - a.shape[1])))
            arrays[f"{net}b{n}"] = np.pad(b, (0, P - b.shape[0]))
    arrays["ar"] = np.repeat(arrays.pop("L3_ffn_adaptive_range"), P)
    arrays["head_blocks"] = np.kron(np.eye(HEADS), np.ones((HD, HD))).astype(np.float32)
    twist, q = np.zeros((P, P), np.float32), np.eye(P // 4, dtype=np.float32)
    for dst, (src, sign) in enumerate(((2, 1), (3, -1), (0, -1), (1, 1))):
        twist[src * 32:src * 32 + 32, dst * 32:dst * 32 + 32] = sign * q
    arrays["twist"] = twist
    dram = {n: nc.dram_tensor(n, a.shape, mybir.dt.from_np(a.dtype), kind="ExternalInput").ap()
            for n, a in arrays.items()}
    shape, dtype = _OUTS[0]
    out = nc.dram_tensor("out", shape, mybir.dt.from_np(np.dtype(dtype)), kind="ExternalOutput").ap()
    build(nc, dram, out)
    r = run_bass_kernel_spmd(nc, [arrays], core_ids=[0])
    return r.results[0]["out"]
```

```python
from contextlib import ExitStack

import concourse.bass as bass
from concourse import mybir

F32 = mybir.dt.float32
F16 = mybir.dt.float16
I32 = mybir.dt.int32
ALU = mybir.AluOpType
ACT = mybir.ActivationFunctionType
AX = mybir.AxisListType

P = 128
BATCH, SEQ, DM = 16, 256, 128
TILES = BATCH * SEQ // P
CHUNK = 512
NCH = BATCH * SEQ // CHUNK
TPC = CHUNK // P
NST = 64
NE = 8
INTER = 256
IT = INTER // P
HEADS, HD = 16, 8
NG = 4
EPS = 1e-5
MASKED = -60000.0


def sl(i, n):
    return bass.ds(i, n)


def spread(ap, dims):
    return bass.AP(tensor=ap.tensor, offset=ap.offset, ap=[list(ap.ap[0])] + dims)


class Program:

    def __init__(self, nc, ctx, dram, out):
        self.nc, self.ctx, self.dram, self.out = nc, ctx, dram, out

        self.stage_sems = ExitStack()
        self.used = []

    def sem(self, name):
        s = self.stage_sems.enter_context(self.nc.semaphore(name))
        self.used.append(s)
        return s

    def end_layer(self):
        with self.nc.Block() as block:

            @block.gpsimd
            def _(pool):
                for s in self.used:
                    pool.sem_clear(s)

        self.stage_sems.close()
        self.used = []

    def sb(self, name, shape, dt=F32, ctx=None):
        return (ctx or self.ctx).enter_context(self.nc.sbuf_tensor(name, shape, dt))



def load(k):
    nc, d = k.nc, k.dram
    arrived = k.sem("inputs_arrived")
    cleared = k.sem("constants_cleared")
    own_arrived, own_loads = k.late[0]
    with nc.Block() as block:

        @block.sync
        def _(sp):
            sp.dma_start(k.x[:], d["L0_attn_x"].rearrange("b (h p) d -> p (b h) d", p=P)).then_inc(arrived, 16)
            for dst, src in own_loads:
                sp.dma_start(dst, src).then_inc(own_arrived, 16)
            sp.wait_ge(arrived, 16)

        @block.gpsimd
        def _(pool):
            pool.memset(k.ident[:], 0.0).then_inc(cleared, 1)
            pool.memset(k.ident16[:], 0.0).then_inc(cleared, 1)
            pool.memset(k.mask_kq[:], 0.0).then_inc(cleared, 1)
            pool.memset(k.mask_qk[:], 0.0).then_inc(cleared, 1)
            pool.memset(k.eps[:], EPS).then_inc(cleared, 1)
            pool.iota(k.lag_i[:], pattern=[[1, SEQ]], base=0, channel_multiplier=0).then_inc(cleared, 1)
            pool.memset(k.mirror[:], 0.0).then_inc(cleared, 1)
            pool.wait_ge(cleared, 7)
            pool.affine_select(out=k.mirror[:], in_=k.mirror[:], compare_op=ALU.not_equal, fill=1.0, base=1 - P,
                               pattern=[[1, P]], channel_multiplier=1)
            for m in (k.ident, k.ident16):
                pool.affine_select(out=m[:], in_=m[:], compare_op=ALU.not_equal, fill=1.0, base=0,
                                   pattern=[[-1, P]], channel_multiplier=1)
            pool.affine_select(out=k.mask_kq[:], in_=k.mask_kq[:], compare_op=ALU.is_ge, fill=MASKED,
                               base=0, pattern=[[0, 4], [1, P]], channel_multiplier=-1)
            pool.affine_select(out=k.mask_qk[:], in_=k.mask_qk[:], compare_op=ALU.is_ge, fill=MASKED,
                               base=0, pattern=[[0, 4], [-1, P]], channel_multiplier=1)
            pool.tensor_copy(k.lag[:], k.lag_i[:])

        @block.vector
        def _(dve):
            dve.memset(k.ps[:], 0.0)



def norm(k, tag, src, chan, z_out=None, loads=(), split=()):
    nc = k.nc
    stats_done, aggr_done, std_done = k.sem(f"{tag}_stats"), k.sem(f"{tag}_aggr"), k.sem(f"{tag}_std")
    rstd_done, z_ready, turned = k.sem(f"{tag}_rstd"), k.sem(f"{tag}_z"), k.sem(f"{tag}_turned")
    bank_free, hi_made = k.sem(f"{tag}_bank_free"), k.sem(f"{tag}_weights_hi")
    st, mv, std, rstd, z = k.st, k.mv, k.std, k.rstd, k.z8
    RING = 8
    with nc.Block() as block:

        @block.gpsimd
        def _(pool):
            for count, name in enumerate(split):
                pool.tensor_copy(k.w_hi[name][:], k.w[name][:]).then_inc(hi_made, 1)
                pool.wait_ge(hi_made, count + 1)
                pool.tensor_tensor(k.w_lo[name][:], k.w[name][:], k.w_hi[name][:], ALU.subtract)

        @block.sync
        def _(sp):
            for arrived, weights in loads:
                for dst, from_dram in weights:
                    sp.dma_start(dst, from_dram).then_inc(arrived, 16)

        @block.vector
        def _(dve):
            for t in range(TILES):
                dve.bn_stats(st[:, t, :], src[:, t, :]).then_inc(stats_done, 1)
            dve.wait_ge(stats_done, TILES)
            for t in range(TILES):
                dve.bn_aggr(mv[:, t, :], st[:, t, :]).then_inc(aggr_done, 1)
            dve.wait_ge(std_done, 1)
            dve.reciprocal(rstd[:], std[:]).then_inc(rstd_done, 1)
            dve.wait_ge(rstd_done, 1)
            for i in range(TILES // RING):
                for m in range(RING):
                    t = i * RING + m
                    if z_out is None:
                        dve.wait_ge(turned, t + 1)
                    dst = z[:, m, :] if z_out is None else z_out[:, t:t + 1, :]
                    dve.tensor_scalar(dst, src[:, t:t + 1, :], mv[:, t:t + 1, 0:1],
                                      rstd[:, t:t + 1], ALU.subtract, ALU.mult).then_inc(z_ready, 1)

        @block.scalar
        def _(act):
            act.wait_ge(aggr_done, TILES)
            act.activation(std[:], mv[:, :, 1], ACT.Sqrt, bias=k.eps[:, 0:1]).then_inc(std_done, 1)
            act.sem_inc(bank_free, 2)
            for i in range(TILES // RING):
                for m in range(2):
                    act.wait_ge(turned, RING + i * RING + 4 * m + 4)
                    act.activation(chan[:, sl(i * 2 * CHUNK + m * CHUNK, CHUNK)], k.ps[:, m, :],
                                   ACT.Copy).then_inc(bank_free, 1)

        @block.tensor
        def _(pe):
            pe.sem_inc(turned, RING)
            if z_out is not None:
                for t in range(TILES):
                    if t % 4 == 0:
                        pe.wait_ge(bank_free, t // 4 + 1)
                    pe.wait_ge(z_ready, t + 1)
                    pe.transpose(k.ps[:, t // 4 % 2, t % 4 * P:t % 4 * P + P], z_out[:, t, :],
                                 k.ident[:]).then_inc(turned, 1)
                return
            for i in range(TILES // RING):
                for m in range(RING):
                    if m % 4 == 0:
                        pe.wait_ge(bank_free, i * 2 + m // 4 + 1)
                    pe.wait_ge(z_ready, i * RING + m + 1)
                    pe.transpose(k.ps[:, m // 4, m % 4 * P:m % 4 * P + P], z[:, m, :],
                                 k.ident[:]).then_inc(turned, 1)



def gates(k, z1, s2, weight):
    nc = k.nc
    prepared, logits_done = k.sem("gate_in"), k.sem("gate_logits")
    step, x_added = k.sem("gate_step"), k.sem("gate_x")
    var_ready, std_ready = k.sem("gate_var2"), k.sem("gate_std2")
    exped = k.sem("gate_exp")
    with ExitStack() as st, nc.Block() as block:
        gs = k.sb("gate_scaled", [P, NE], ctx=st)
        bias = k.sb("gate_bias", [P, P], ctx=st)
        v2, std2 = k.sb("gate_v2", [P, TILES], ctx=st), k.sb("gate_std2_sb", [P, TILES], ctx=st)
        lg = k.ps[:, 7, 0:TILES * NE].rearrange("p (t e) -> p t e", e=NE)
        lb = k.ps[:, 6, 0:NE]
        pr = k.sb("gate_p", [P, TILES, NE], ctx=st)
        red = k.sb("gate_red", [P, TILES], ctx=st)
        inv = k.sb("gate_inv", [P, TILES], ctx=st)
        cmp1 = k.sb("gate_cmp1", [P, TILES, NE, NE], ctx=st)
        cmp2 = k.sb("gate_cmp2", [P, TILES, NE, NE], ctx=st)
        earlier = k.sb("gate_earlier", [P, NE, NE], ctx=st)
        made = k.sem("gate_earlier_made")

        @block.gpsimd
        def _(pool):
            pool.memset(earlier[:], 1.0).then_inc(made, 1)
            pool.wait_ge(made, 1)
            pool.affine_select(out=earlier[:], in_=earlier[:], compare_op=ALU.is_gt, fill=0.0, base=0,
                               pattern=[[1, NE], [-1, NE]], channel_multiplier=0).then_inc(made, 1)
            pool.tensor_tensor(k.x[:], k.x[:], z1[:], ALU.add).then_inc(x_added, 1)
            pool.wait_ge(x_added, 1)
            pool.tensor_tensor(k.x[:], k.x[:], k.w["b_out"][:].unsqueeze(1).to_broadcast([P, TILES, DM]), ALU.add)

        @block.scalar
        def _(act):
            for n in "gu":
                act.activation(k.w_hi[n][:], k.w["W" + n][:], ACT.Copy)
            act.wait_ge(var_ready, 2)
            act.activation(std2[:], v2[:], ACT.Sqrt, bias=k.eps[:, 0:1]).then_inc(std_ready, 1)
            act.wait_ge(step, 4)
            act.activation(pr[:], pr[:], ACT.Exp).then_inc(exped, 1)

        @block.tensor
        def _(pe):
            pe.wait_ge(prepared, 2)
            for t in range(TILES):
                ins = pe.matmul(lg[:, t, :], k.xT[:, t * P:t * P + P], gs[:], start=True, stop=True)
            ins = pe.matmul(lb, bias[:], k.w["gate"][:], start=True, stop=True)
            ins.then_inc(logits_done, 1)

        @block.vector
        def _(dve):
            n = 0

            def link(ins):
                nonlocal n
                n += 1
                ins.then_inc(step, 1)
                dve.wait_ge(step, n)

            def rows(a):
                return a[:].unsqueeze(2).to_broadcast([P, TILES, NE])

            dve.tensor_scalar(gs[:], k.w["gate"][:], k.w["ffn_scale"][:, 0:1], None, ALU.mult).then_inc(prepared, 1)
            dve.tensor_copy(bias[:], k.w["ffn_bias"][:].to_broadcast([P, P])).then_inc(prepared, 1)
            dve.tensor_tensor(v2[:], k.rstd[:], k.rstd[:], ALU.mult).then_inc(var_ready, 1)
            dve.wait_ge(var_ready, 1)
            dve.tensor_tensor(v2[:], v2[:], k.mv[:, :, 1], ALU.mult).then_inc(var_ready, 1)
            dve.wait_ge(std_ready, 1)
            dve.reciprocal(s2[:], std2[:]).then_inc(var_ready, 1)
            dve.wait_ge(var_ready, 3)
            dve.wait_ge(logits_done, 1)
            link(dve.tensor_tensor(pr[:], lg, rows(s2), ALU.mult))
            link(dve.tensor_tensor(pr[:], pr[:], lb.unsqueeze(1).to_broadcast([P, TILES, NE]), ALU.add))
            link(dve.tensor_reduce(red[:], pr[:], AX.X, ALU.max))
            link(dve.tensor_tensor(pr[:], pr[:], rows(red), ALU.subtract))
            dve.wait_ge(exped, 1)
            dve.wait_ge(made, 2)
            link(dve.tensor_reduce(red[:], pr[:], AX.X, ALU.add))
            link(dve.reciprocal(inv[:], red[:]))
            link(dve.tensor_tensor(pr[:], pr[:], rows(inv), ALU.mult))
            own = pr[:].unsqueeze(3).to_broadcast([P, TILES, NE, NE])
            other = pr[:].unsqueeze(2).to_broadcast([P, TILES, NE, NE])
            dve.tensor_tensor(cmp1[:], other, own, ALU.is_gt)
            link(dve.tensor_tensor(cmp2[:], other, own, ALU.is_equal))
            link(dve.tensor_tensor(cmp2[:], cmp2[:], earlier[:].unsqueeze(1).to_broadcast([P, TILES, NE, NE]),
                                   ALU.mult))
            link(dve.tensor_tensor(cmp1[:], cmp1[:], cmp2[:], ALU.add))
            link(dve.tensor_reduce(weight[:], cmp1[:], AX.X, ALU.add))
            link(dve.scalar_tensor_tensor(out=pr[:], in0=weight[:], scalar=1.5, in1=pr[:], op0=ALU.is_lt,
                                          op1=ALU.mult))
            link(dve.tensor_reduce(red[:], pr[:], AX.X, ALU.add))
            link(dve.tensor_scalar(red[:], red[:], EPS, None, ALU.add))
            link(dve.reciprocal(inv[:], red[:]))
            link(dve.tensor_tensor(weight[:], pr[:], rows(inv), ALU.mult))



def ssm_kernel(k, z1, s2, u):
    nc, w = k.nc, k.w
    step, exps, e_ready, e_used = k.sem("ssm_step"), k.sem("ssm_pre"), k.sem("ssm_e"), k.sem("ssm_e_used")
    stored, zeroed = k.sem("ssm_stored"), k.sem("ssm_zeroed")
    u_step, u_mirrored, u_stored = k.sem("ssm_u"), k.sem("ssm_u_mirrored"), k.sem("ssm_u_stored")
    scaled = k.sem("ssm_scaled")
    UNROLL = 16
    NU = 2 * DM * BATCH // CHUNK
    flat = u[:].rearrange("p h d b -> p (h d b)")
    with ExitStack() as st, nc.Block() as block:
        dt = k.sb("ssm_dt", [P, 1], ctx=st)
        ea = k.sb("ssm_ea", [P, NST], ctx=st)
        nr = k.sb("ssm_nr", [P, NST], ctx=st)
        cb = k.sb("ssm_cb", [P, NST], ctx=st)
        e = k.sb("ssm_e", [P, 4, SEQ], ctx=st)
        kn = k.sb("ssm_k", [P, 4, SEQ], ctx=st)
        zero = k.sb("ssm_zero", [P, P], ctx=st)

        @block.scalar
        def _(act):
            act.activation(dt[:], w["log_dt"][:], ACT.Exp).then_inc(exps, 1)
            act.activation(ea[:], w["log_A"][:], ACT.Exp).then_inc(exps, 1)
            act.wait_ge(step, 2)
            with act.Fori(0, NST // UNROLL) as i:
                for m in range(UNROLL):
                    act.wait_ge(e_used, i * UNROLL + m + 1)
                    act.activation(e[:, m % 4, :], k.lag[:], ACT.Exp, scale=nr[:, sl(i * UNROLL + m, 1)]).then_inc(e_ready, 1)
            for c in range(NU):
                act.wait_ge(u_mirrored, c + 1)
                act.activation(flat[:, c * CHUNK:(c + 1) * CHUNK], k.ps[:, c, :], ACT.Copy).then_inc(u_stored, 1)
            act.wait_ge(u_stored, NU)

        @block.tensor
        def _(pe):
            for c in range(NU):
                pe.wait_ge(u_step, 1 if c < NU // 2 else 2)
                pe.matmul(k.ps[:, c, :], k.mirror[:], flat[:, c * CHUNK:(c + 1) * CHUNK],
                          start=True, stop=True).then_inc(u_mirrored, 1)

        @block.gpsimd
        def _(pool):
            pool.memset(zero[:], 0.0).then_inc(zeroed, 1)
            be = w["beta"][:].unsqueeze(1).to_broadcast([P, BATCH, DM])
            for h in range(2):
                pool.wait_ge(scaled, TILES // 2 * (h + 1))
                src = z1[:].rearrange("p (b h) d -> p b h d", h=2)[:, :, h, :]
                pool.tensor_tensor(u[:, h].rearrange("p d b -> p b d"), src, be, ALU.add).then_inc(u_step, 1)
            for n in "gu":
                pool.tensor_tensor(k.w_lo[n][:], w["W" + n][:], k.w_hi[n][:], ALU.subtract)

        @block.vector
        def _(dve):
            for h in range(2):
                for b in range(BATCH):
                    t = 2 * b + h
                    dve.scalar_tensor_tensor(out=z1[:, t, :], in0=z1[:, t, :], scalar=s2[:, t:t + 1], in1=w["gamma"][:],
                                             op0=ALU.mult, op1=ALU.mult).then_inc(scaled, 1)
            dve.wait_ge(exps, 2)
            dve.tensor_scalar(nr[:], ea[:], dt[:, 0:1], -1.0, ALU.mult, ALU.mult).then_inc(step, 1)
            dve.scalar_tensor_tensor(out=cb[:], in0=w["B"][:], scalar=dt[:, 0:1], in1=w["C"][:],
                                     op0=ALU.mult, op1=ALU.mult).then_inc(step, 1)
            dve.memset(kn[:], 0.0).then_inc(step, 1)
            dve.wait_ge(step, 3)
            dve.sem_inc(e_used, 4)
            with dve.Fori(0, NST // UNROLL) as i:
                for m in range(UNROLL):
                    dve.wait_ge(e_ready, i * UNROLL + m + 1)
                    dve.wait_ge(e_used, i * UNROLL + m + 1)
                    dve.scalar_tensor_tensor(out=kn[:, m % 4, :], in0=e[:, m % 4, :], scalar=cb[:, sl(i * UNROLL + m, 1)],
                                             in1=kn[:, m % 4, :], op0=ALU.mult, op1=ALU.add).then_inc(e_used, 1)
            dve.wait_ge(e_used, NST + 4)
            dve.tensor_tensor(kn[:, 0:2, :], kn[:, 0:2, :], kn[:, 2:4, :], ALU.add).then_inc(step, 1)
            dve.wait_ge(step, 4)
            dve.tensor_tensor(kn[:, 0, :], kn[:, 0, :], kn[:, 1, :], ALU.add).then_inc(step, 1)
            dve.wait_ge(step, 5)
            dve.tensor_tensor(kn[:, 0, 0:1], kn[:, 0, 0:1], w["D"][:], ALU.add).then_inc(step, 1)

        @block.sync
        def _(sp):
            sp.wait_ge(zeroed, 1)
            sp.dma_start(k.kpad[:, 0:P], zero[:]).then_inc(stored, 16)
            sp.wait_ge(step, 6)
            sp.dma_start(k.kpad[:, P:P + SEQ], kn[:, 0, :]).then_inc(stored, 16)
            sp.wait_ge(stored, 32)


def convolve(k, u):
    nc = k.nc
    t_in = [k.sem(f"conv_toeplitz{m}") for m in range(2)]
    u_copied, used = k.sem("conv_u"), k.sem("conv_used")
    y_free, stored = k.sem("conv_y_free"), [k.sem(f"conv_stored{m}") for m in range(2)]
    CH = 8
    STEPS = DM // CH
    yv = k.yT.rearrange("(s g j) b t -> s j b g t", g=2, j=4)
    with ExitStack() as st, nc.Block() as block:
        toe = k.sb("toeplitz", [P, 2, CH, SEQ], ctx=st)
        uc = k.sb("conv_uc", [P, 2, 2, CH, BATCH], ctx=st)
        y = k.sb("conv_ysb", [P, 2, 2, SEQ], ctx=st)

        @block.sync
        def _(sp):
            with sp.Fori(0, STEPS // 2) as i:
                for m in range(2):
                    s = i * 2 + m
                    sp.wait_ge(used, s + 1)
                    src = bass.AP(tensor=k.kpad.tensor, offset=s * (CH * (P + SEQ)) + 1,
                                  ap=[[1, P], [P + SEQ, CH], [1, SEQ]])
                    sp.dma_start(toe[:, m], src).then_inc(t_in[m], 16)

        @block.gpsimd
        def _(pool):
            with pool.Fori(0, STEPS // 2) as i:
                for m in range(2):
                    s = i * 2 + m
                    pool.wait_ge(used, s + 1)
                    pool.tensor_copy(uc[:, m], u[:, :, sl(s * CH, CH), :]).then_inc(u_copied, 1)

        @block.tensor
        def _(pe):
            pe.sem_inc(used, 2)
            with pe.Fori(0, STEPS // 2) as i:
                for m in range(2):
                    s = i * 2 + m
                    pe.wait_ge(t_in[m], i * 16 + 16)
                    pe.wait_ge(u_copied, s + 1)
                    pe.wait_ge(y_free, s + 1)
                    for c in range(CH):
                        g, j = c // 4, c % 4
                        o = k.ps[32 * j:32 * j + BATCH, m, g * SEQ:g * SEQ + SEQ]
                        pe.matmul(o, uc[:, m, 0, c, :], toe[:, m, c, :], start=True, stop=False,
                                  skip_group_check=True)
                        ins = pe.matmul(o[:, P:SEQ], uc[:, m, 1, c, :], toe[:, m, c, 0:P], start=False, stop=True,
                                        skip_group_check=True)
                    ins.then_inc(used, 1)

        @block.vector
        def _(dve):
            dve.sem_inc(y_free, 2)
            with dve.Fori(0, STEPS // 2) as i:
                for m in range(2):
                    s = i * 2 + m
                    dve.wait_ge(used, s + 3)
                    dve.wait_ge(stored[m], i * 64 + 64)
                    dve.tensor_copy(y[:, m].rearrange("p g t -> p (g t)"), k.ps[:, m, :]).then_inc(y_free, 1)

        @block.scalar
        def _(act):
            for m in range(2):
                act.sem_inc(stored[m], 64)
            with act.Fori(0, STEPS // 2) as i:
                for m in range(2):
                    s = i * 2 + m
                    act.wait_ge(y_free, s + 3)
                    for j in range(4):
                        act.dma_start(yv[sl(s, 1), j], y[32 * j:32 * j + BATCH, m]).then_inc(stored[m], 16)
            for m in range(2):
                act.wait_ge(stored[m], 64 + STEPS // 2 * 64)



def experts(k, xT, weight):
    nc, w = k.nc, k.w
    PAIRS, N = (NE + 1) * IT, NE + 1
    gate_mm, up_mm, sg_ready, h_ready = k.sem("ex_gate"), k.sem("ex_up"), k.sem("ex_silu"), k.sem("ex_h")
    down_mm, acc_done, y_in, y_used = k.sem("ex_down"), k.sem("ex_acc"), k.sem("ex_y"), k.sem("ex_y_used")
    hi_done, lo_done = k.sem("ex_xh"), k.sem("ex_xl")
    GB, UB, OB = (0, 1), (2, 3), (4, 5, 6)
    with ExitStack() as st, nc.Block() as block:
        sg = k.sb("ex_sg", [P, 2, CHUNK], ctx=st)
        h = k.sb("ex_h_sb", [P, 3, IT, CHUNK], ctx=st)
        y = k.sb("ex_y_sb", [P, CHUNK], ctx=st)
        xh, xl = k.sb("ex_x_hi", [P, BATCH * SEQ], F16, ctx=st), k.sb("ex_x_lo", [P, BATCH * SEQ], F16, ctx=st)

        @block.gpsimd
        def _(pool):
            with pool.Fori(0, NCH) as i:
                at = sl(i * CHUNK, CHUNK)
                pool.tensor_copy(xh[:, at], xT[:, at]).then_inc(hi_done, 1)
                pool.wait_ge(hi_done, i + 1)
                pool.tensor_tensor(xl[:, at], xT[:, at], xh[:, at], ALU.subtract).then_inc(lo_done, 1)

        @block.sync
        def _(sp):
            with sp.Fori(0, NCH) as i:
                sp.wait_ge(y_used, i + 1)
                sp.dma_start(y[:].rearrange("d (b t) -> d b t", b=2), k.yT[:, sl(i * 2, 2), :]).then_inc(y_in, 16)

        @block.tensor
        def _(pe):
            pe.sem_inc(y_used, 1)
            with pe.Fori(0, NCH // 2) as j:
                for i in (j * 2, j * 2 + 1):
                    def product(bank, n, e, it):
                        at = sl(i * CHUNK, CHUNK)
                        hi, lo = (part[n][:, e, it * P:it * P + P] for part in (k.w_hi, k.w_lo))
                        pe.matmul(k.ps[:, bank, :], hi, xh[:, at], start=True, stop=False)
                        pe.matmul(k.ps[:, bank, :], hi, xl[:, at], start=False, stop=False)
                        return pe.matmul(k.ps[:, bank, :], lo, xh[:, at], start=False, stop=True)

                    def gate_up(e):
                        if e == 0:
                            pe.wait_ge(hi_done, i + 1)
                            pe.wait_ge(lo_done, i + 1)
                        for it in range(IT):
                            n = e * IT + it
                            pe.wait_ge(sg_ready, i * PAIRS + n + 1)
                            product(GB[n % 2], "g", e, it).then_inc(gate_mm, 1)
                            pe.wait_ge(h_ready, i * PAIRS + n + 1)
                            product(UB[n % 2], "u", e, it).then_inc(up_mm, 1)

                    def down(e):
                        pe.wait_ge(acc_done, i * N + e + 1)
                        if e == NE:
                            pe.wait_ge(y_in, i * 16 + 16)
                            for t in range(TPC):
                                ins = pe.matmul(k.ps[:, OB[e % 3], t * P:t * P + P], y[:, t * P:t * P + P],
                                                w["W_out"][:], start=(t == 0), stop=False, skip_group_check=True)
                            ins.then_inc(y_used, 1)
                        pe.wait_ge(h_ready, 2 + i * PAIRS + (e + 1) * IT)
                        for t in range(TPC):
                            for it in range(IT):
                                ins = pe.matmul(k.ps[:, OB[e % 3], t * P:t * P + P], h[:, e % 3, it, t * P:t * P + P],
                                                w["Wd"][:, e, it, :], start=(it == 0 and e < NE), stop=(it == IT - 1),
                                                skip_group_check=True)
                        ins.then_inc(down_mm, 1)

                    for e in range(N):
                        gate_up(e)
                        if e:
                            down(e - 1)
                    down(NE)

        @block.scalar
        def _(act):
            act.sem_inc(sg_ready, 2)
            with act.Fori(0, NCH // 2) as j:
                for i in (j * 2, j * 2 + 1):
                    for n in range(PAIRS):
                        act.wait_ge(gate_mm, i * PAIRS + n + 1)
                        act.wait_ge(h_ready, i * PAIRS + n + 1)
                        act.activation(sg[:, n % 2, :], k.ps[:, GB[n % 2], :], ACT.Silu).then_inc(sg_ready, 1)

        @block.vector
        def _(dve):
            dve.sem_inc(h_ready, 2)
            dve.sem_inc(acc_done, 3)
            with dve.Fori(0, NCH // 2) as j:
                for i in (j * 2, j * 2 + 1):
                    def gated(e):
                        dve.wait_ge(acc_done, i * N + e + 1)
                        for it in range(IT):
                            n = e * IT + it
                            dve.wait_ge(sg_ready, 2 + i * PAIRS + n + 1)
                            dve.wait_ge(up_mm, i * PAIRS + n + 1)
                            dve.tensor_tensor(h[:, e % 3, it, :], sg[:, n % 2, :], k.ps[:, UB[n % 2], :],
                                              ALU.mult).then_inc(h_ready, 1)

                    def add(e):
                        dve.wait_ge(down_mm, i * N + e + 1)
                        dve.wait_ge(acc_done, i * N + e + 3)
                        if e < NE:
                            for t in range(TPC):
                                T = i * TPC + t
                                xt = k.x[:, sl(T, 1), :]
                                ins = dve.scalar_tensor_tensor(
                                    out=xt, in0=k.ps[:, OB[e % 3], t * P:t * P + P].unsqueeze(1),
                                    scalar=weight[:, sl(T, 1), e:e + 1].rearrange("p a b -> p (a b)"), in1=xt,
                                    op0=ALU.mult, op1=ALU.add)
                        else:
                            xc = k.x[:, sl(i * TPC, TPC), :]
                            ins = dve.tensor_tensor(xc, xc, k.ps[:, OB[e % 3], :].rearrange("p (t c) -> p t c", c=P),
                                                    ALU.add)
                        ins.then_inc(acc_done, 1)

                    for e in range(N):
                        gated(e)
                        if e > 1:
                            add(e - 2)
                    add(N - 2)
                    add(N - 1)




ROWS = 4


def project(k, tag, xT, wq, wk, wv, bo):
    nc = k.nc
    x_copied, qk_mm, v_mm = k.sem(f"{tag}_xc"), k.sem(f"{tag}_qk"), k.sem(f"{tag}_v")
    hi_done, lo_done, v_done = k.sem(f"{tag}_hi"), k.sem(f"{tag}_lo"), k.sem(f"{tag}_vd")
    stored = [k.sem(f"{tag}_st{m}") for m in range(2)]
    const_set, const_stored = k.sem(f"{tag}_cs"), k.sem(f"{tag}_cst")
    with ExitStack() as st, nc.Block() as block:
        xc = k.sb(f"{tag}_x", [P, 2, CHUNK], ctx=st)
        hi = k.sb(f"{tag}_hi_sb", [P, 2, 2, CHUNK], F16, ctx=st)
        lo = k.sb(f"{tag}_lo_sb", [P, 2, 2, CHUNK], F16, ctx=st)
        const = k.sb(f"{tag}_const", [P, 2, SEQ], F16, ctx=st)

        @block.gpsimd
        def _(pool):
            pool.memset(const[:, 0, :], 0.0).then_inc(const_set, 1)
            pool.memset(const[:, 1, :], 1.0).then_inc(const_set, 1)
            with pool.Fori(0, NCH // 2) as j:
                for m in range(2):
                    pool.wait_ge(v_mm, j * 2 + m + 1)
                    pool.tensor_copy(xc[:, m], xT[:, sl(j * 2 * CHUNK + m * CHUNK, CHUNK)]).then_inc(x_copied, 1)
            if bo is not None:
                pool.tensor_tensor(k.x[:], k.x[:], bo[:].unsqueeze(1).to_broadcast([P, TILES, DM]), ALU.add)

        @block.tensor
        def _(pe):
            pe.sem_inc(v_mm, 2)
            with pe.Fori(0, NCH // 2) as j:
                for m, i in ((0, j * 2), (1, j * 2 + 1)):
                    for n, w in enumerate((wq, wk)):
                        pe.wait_ge(lo_done, i * 2 + n + 1)
                        pe.matmul(k.ps[:, n, :], w[:], xT[:, sl(i * CHUNK, CHUNK)], start=True,
                                  stop=True).then_inc(qk_mm, 1)
                    pe.wait_ge(v_done, i + 1)
                    pe.wait_ge(x_copied, i + 1)
                    for t in range(TPC):
                        ins = pe.matmul(k.ps[:, 2, t * P:t * P + P], xc[:, m, t * P:t * P + P], wv[:], start=True, stop=True)
                    ins.then_inc(v_mm, 1)

        @block.scalar
        def _(act):
            with act.Fori(0, NCH // 2) as j:
                for m, i in ((0, j * 2), (1, j * 2 + 1)):
                    for n in range(2):
                        act.wait_ge(qk_mm, i * 2 + n + 1)
                        act.wait_ge(stored[m], j * 96 + 96)
                        act.activation(hi[:, m, n, :], k.ps[:, n, :], ACT.Copy).then_inc(hi_done, 1)

        @block.vector
        def _(dve):
            dve.sem_inc(lo_done, 2)
            dve.sem_inc(v_done, 1)
            with dve.Fori(0, NCH // 2) as j:
                for m, i in ((0, j * 2), (1, j * 2 + 1)):
                    for n in range(2):
                        dve.wait_ge(hi_done, i * 2 + n + 1)
                        dve.wait_ge(stored[m], j * 96 + 96)
                        dve.tensor_tensor(lo[:, m, n, :], k.ps[:, n, :], hi[:, m, n, :], ALU.subtract).then_inc(lo_done, 1)
                    dve.wait_ge(v_mm, i + 3)
                    dve.tensor_copy(k.v[:, sl(i * TPC, TPC), :], k.ps[:, 2, :].rearrange("p (t c) -> p t c", c=P)
                                    ).then_inc(v_done, 1)

        @block.sync
        def _(sp):
            for m in range(2):
                sp.sem_inc(stored[m], 96)
            sp.wait_ge(const_set, 2)
            zeros = const[:, 0, :].unsqueeze(1).to_broadcast([P, BATCH, SEQ])
            for dst in (k.qs, k.ks):
                sp.dma_start(dst[:, :, 3, :].rearrange("b c t -> c b t"), zeros).then_inc(const_stored, 16)
            sp.wait_ge(const_stored, 32)
            ones = const[0:HEADS, 1, :].unsqueeze(1).to_broadcast([HEADS, BATCH, SEQ])
            sp.dma_start(k.ks[:, 0:P:HD, 3, :].rearrange("b c t -> c b t"), ones).then_inc(const_stored, 16)
            with sp.Fori(0, NCH // 2) as j:
                for m in range(2):
                    sp.wait_ge(lo_done, j * 4 + 2 * m + 4)
                    for dst, n, parts in ((k.qs, 0, (hi, hi, lo)), (k.ks, 1, (hi, lo, hi))):
                        for r, part in enumerate(parts):
                            sp.dma_start(dst[sl(j * 4 + 2 * m, 2), :, r, :].rearrange("b c t -> c b t"),
                                         part[:, m, n, :].rearrange("p (b t) -> p b t", b=2)).then_inc(stored[m], 16)
            for m in range(2):
                sp.wait_ge(stored[m], NCH // 2 * 96 + 96)
            sp.wait_ge(const_stored, 48)


def attend(k, tag, wo):
    nc = k.nc
    scale = 1.0 / float(HD) ** 0.5
    BLK = [(0, 0), (1, 0), (1, 1)]
    s_mm, s_free, t_mm, p_ready = k.sem(f"{tag}_s"), k.sem(f"{tag}_sf"), k.sem(f"{tag}_t"), k.sem(f"{tag}_p")
    pv_mm, cx_ready, neg_ready, mt_mm = k.sem(f"{tag}_pv"), k.sem(f"{tag}_cx"), k.sem(f"{tag}_ng"), k.sem(f"{tag}_mt")
    m_copied, m_stored = k.sem(f"{tag}_mc"), k.sem(f"{tag}_ms")
    s_in = [k.sem(f"{tag}_sin{m}") for m in range(2)]
    t_in = [k.sem(f"{tag}_tin{m}") for m in range(2)]
    v_set, v_copied, blk_set = k.sem(f"{tag}_vs"), k.sem(f"{tag}_vc"), k.sem(f"{tag}_bs")
    ct_mm, den_done, norm_done, back_mm = k.sem(f"{tag}_ct"), k.sem(f"{tag}_dn"), k.sem(f"{tag}_nd"), k.sem(f"{tag}_bk")
    back_copied, o_mm, x_added = k.sem(f"{tag}_bc"), k.sem(f"{tag}_o"), k.sem(f"{tag}_xa")
    S_B, T_B, PV_B, CT_B, MISC_B = (0, 1), (2, 3), (4, 5), 6, 7
    with ExitStack() as st, nc.Block() as block:
        qst = [k.sb(f"{tag}_qst{m}", [P, NG, SEQ], F16, ctx=st) for m in range(2)]
        kst = [k.sb(f"{tag}_kst{m}", [P, NG, SEQ], F16, ctx=st) for m in range(2)]
        qbl = [k.sb(f"{tag}_qbl{m}", [P, NG, 4, SEQ], F16, ctx=st) for m in range(2)]
        kbl = [k.sb(f"{tag}_kbl{m}", [P, NG, 4, SEQ], F16, ctx=st) for m in range(2)]
        va = [k.sb(f"{tag}_va{m}", [P, 2, HEADS, 32], ctx=st) for m in range(2)]
        p0 = k.sb(f"{tag}_p0", [P, NG, 4, SEQ], ctx=st)
        p1 = k.sb(f"{tag}_p1", [P, NG, 4, P], ctx=st)
        mx = k.sb(f"{tag}_mx", [P, 3, HEADS], ctx=st)
        neg = k.sb(f"{tag}_neg", [P, 2, HEADS], ctx=st)
        mT = k.sb(f"{tag}_mT", [HEADS, SEQ], F16, ctx=st)
        cx = k.sb(f"{tag}_cx_sb", [P, 2, NG, SEQ], ctx=st)
        rden = k.sb(f"{tag}_rden", [P, 2, HEADS], ctx=st)
        cn = k.sb(f"{tag}_cn", [P, 2, DM], ctx=st)
        cT = k.sb(f"{tag}_cT", [P, SEQ], ctx=st)

        def b_of(batch):
            return batch[0] * 2 + batch[1]

        def steps(engine, step):
            def of(s):
                return (s // 2, s % 2) if 0 <= s < BATCH else None

            for s in range(4):
                step(of(s), of(s - 1), of(s - 2), of(s - 3))
            with engine.Fori(0, BATCH // 2 - 2) as j:
                step((j + 2, 0), (j + 1, 1), (j + 1, 0), (j, 1))
                step((j + 2, 1), (j + 2, 0), (j + 1, 1), (j + 1, 0))
            for s in range(BATCH, BATCH + 3):
                step(None, of(s - 1), of(s - 2), of(s - 3))

        @block.sync
        def _(sp):
            def load_scores(batch):
                b, m = b_of(batch), batch[1]
                src = k.qs[sl(b, 1)].rearrange("b (g c) r t -> (b c r) g t", g=NG)
                k_src = k.ks[sl(b, 1)].rearrange("b (g c) r t -> (b c r) g t", g=NG)
                sp.wait_ge(s_mm, b * 12 + 1)
                sp.dma_start(qst[m][:], src).then_inc(s_in[m], 16)
                for q in range(4):
                    sp.dma_start(kbl[m][32 * q:32 * q + 32, :, q, :], k_src[32 * q:32 * q + 32]).then_inc(s_in[m], 16)

            def load_k(batch):
                b, m = b_of(batch), batch[1]
                sp.wait_ge(t_mm, b * 12 + 1)
                src = k.ks[sl(b, 1)].rearrange("b (g c) r t -> (b c r) g t", g=NG)
                sp.dma_start(kst[m][:], src).then_inc(t_in[m], 16)

            def load_q(batch):
                b, m = b_of(batch), batch[1]
                src = k.qs[sl(b, 1)].rearrange("b (g c) r t -> (b c r) g t", g=NG)
                sp.wait_ge(m_stored, b * 16 + 16)
                for q in range(4):
                    sp.dma_start(qbl[m][32 * q:32 * q + 32, :, q, :], src[32 * q:32 * q + 32]).then_inc(t_in[m], 16)

            def step(new, mid, old, done):
                if new is not None and not (isinstance(new[0], int) and new == (0, 0)):
                    load_scores(new)
                if mid is not None:
                    b = b_of(mid)
                    load_k(mid)
                    sp.wait_ge(m_copied, b + 1)
                    sp.dma_start(k.qs[sl(b, 1), 0:P:HD, 3, :].rearrange("b c t -> (b c) t"),
                                 mT[:]).then_inc(m_stored, 16)
                    load_q(mid)

            sp.wait_ge(blk_set, 4)
            load_scores((0, 0))
            steps(sp, step)

        @block.gpsimd
        def _(pool):
            for m in range(2):
                pool.memset(qbl[m][:], 0.0).then_inc(blk_set, 1)
                pool.memset(kbl[m][:], 0.0).then_inc(blk_set, 1)
            for m in range(2):
                pool.memset(va[m][:], 0.0).then_inc(v_set, 1)
            pool.wait_ge(v_set, 2)
            for m in range(2):
                pool.memset(va[m][:, :, :, HD:HD + 1], 1.0).then_inc(v_set, 1)
            pool.wait_ge(v_set, 4)

            def copy_v(batch):
                b = b_of(batch)
                pool.wait_ge(pv_mm, b * NG + 1)
                pool.tensor_copy(va[batch[1]][:, :, :, 0:HD],
                                 k.v[:, sl(b * 2, 2), :].rearrange("p t (h d) -> p t h d", d=HD)
                                 ).then_inc(v_copied, 1)

            def step(new, mid, old, done):
                if old is not None:
                    copy_v(old)

            steps(pool, step)

        @block.tensor
        def _(pe):
            pe.sem_inc(s_mm, 13)
            pe.sem_inc(t_mm, 13)
            pe.sem_inc(pv_mm, NG + 1)
            pe.sem_inc(mt_mm, 1)
            pe.sem_inc(back_mm, 1)
            pe.sem_inc(o_mm, 1)
            pe.sem_inc(ct_mm, 3)
            pe.wait_ge(v_set, 4)

            def scores(batch, g, block):
                h, m = batch
                qt, kt = BLK[block]
                n = g * 3 + block
                pe.wait_ge(s_free, b_of(batch) * 12 + n + 1)
                o = k.ps[:, S_B[n % 2], :]
                ins = pe.matmul(o, qst[m][:, g, qt * P:qt * P + P], kbl[m][:, g, :, kt * P:kt * P + P],
                                start=True, stop=(qt != kt))
                if qt == kt:
                    ins = pe.matmul(o, k.ident16[:], k.mask_qk[:], start=False, stop=True)
                ins.then_inc(s_mm, 1)

            def scores_T(batch, g, block):
                h, m = batch
                qt, kt = BLK[block]
                n = g * 3 + block
                pe.wait_ge(p_ready, b_of(batch) * 12 + n + 1)
                o = k.ps[:, T_B[n % 2], :]
                ins = pe.matmul(o, kst[m][:, g, kt * P:kt * P + P], qbl[m][:, g, :, qt * P:qt * P + P],
                                start=True, stop=(qt != kt))
                if qt == kt:
                    ins = pe.matmul(o, k.ident16[:], k.mask_kq[:], start=False, stop=True)
                ins.then_inc(t_mm, 1)

            def values(batch, g):
                h, m = batch
                pe.wait_ge(p_ready, 2 + b_of(batch) * 12 + g * 3 + 3)
                pe.wait_ge(cx_ready, b_of(batch) * NG + g + 1)
                for j in range(4):
                    o = k.ps[32 * j:32 * j + 32, PV_B[g % 2], 0:SEQ]
                    pe.matmul(o, va[m][:, 0, 4 * g + j, :], p0[:, g, j, :], start=True, stop=False)
                    ins = pe.matmul(o[:, P:SEQ], va[m][:, 1, 4 * g + j, :], p1[:, g, j, :], start=False, stop=True)
                ins.then_inc(pv_mm, 1)

            def turn_max(batch, alone):
                b = b_of(batch)
                pe.wait_ge(neg_ready, b + 1)
                if not alone:
                    pe.wait_ge(back_copied, b - 1)
                for qt in range(2):
                    ins = pe.transpose(k.ps[0:HEADS, MISC_B, qt * P:qt * P + P], neg[:, qt, :], k.ident[:])
                ins.then_inc(mt_mm, 1)

            def turn_values(batch, qt):
                b = b_of(batch)
                pe.wait_ge(cx_ready, 2 + b * NG + 4)
                if qt == 0:
                    pe.wait_ge(x_added, b + 1)
                else:
                    pe.wait_ge(norm_done, b * 2 + 1)
                for g in range(NG):
                    ins = pe.transpose(k.ps[:, CT_B, g * P:g * P + P], cx[:, batch[1], g, qt * P:qt * P + P], k.ident[:])
                ins.then_inc(ct_mm, 1)

            def turn_back(batch, max_copied):
                b = b_of(batch)
                if max_copied:
                    pe.wait_ge(m_copied, b + 3)
                for qt in range(2):
                    pe.wait_ge(norm_done, b * 2 + qt + 1)
                    ins = pe.transpose(k.ps[:, MISC_B, SEQ + qt * P:SEQ + qt * P + P], cn[:, qt, :], k.ident[:])
                ins.then_inc(back_mm, 1)

            def output(batch):
                b = b_of(batch)
                pe.wait_ge(back_copied, b + 2)
                for qt in range(2):
                    ins = pe.matmul(k.ps[:, CT_B, qt * P:qt * P + P], cT[:, qt * P:qt * P + P], wo[:],
                                    start=True, stop=True)
                ins.then_inc(o_mm, 1)

            def step(new, mid, old, done):
                for g in range(NG):
                    if g == 0 and new is not None:
                        pe.wait_ge(s_in[new[1]], new[0] * 80 + 80)
                    if g == 0 and old is not None:
                        pe.wait_ge(t_in[old[1]], old[0] * 80 + 80)
                        pe.wait_ge(v_copied, b_of(old) + 1)
                    for block in range(2):
                        if new is not None:
                            scores(new, g, block)
                        if old is not None:
                            scores_T(old, g, block)
                    if mid is not None and g == 0:
                        turn_max(mid, mid in ((0, 0), (0, 1), (1, 0)) if isinstance(mid[0], int) else False)
                    if done is not None:
                        if g == 0:
                            values(done, NG - 1)
                        elif g < 3:
                            turn_values(done, g - 1)
                        else:
                            turn_back(done, mid is not None)
                    if new is not None:
                        scores(new, g, 2)
                    if old is not None:
                        if g:
                            values(old, g - 1)
                        scores_T(old, g, 2)
                if done is not None:
                    output(done)

            steps(pe, step)

        @block.scalar
        def _(act):
            act.sem_inc(p_ready, 2)
            act.sem_inc(back_copied, 1)

            def step(new, mid, old, done):
                if mid is not None:
                    b = b_of(mid)
                    act.wait_ge(mt_mm, b + 2)
                    if not (isinstance(b, int) and b == 0):
                        act.wait_ge(m_stored, b * 16)
                    act.activation(mT[:], k.ps[0:HEADS, MISC_B, 0:SEQ], ACT.Copy).then_inc(m_copied, 1)
                for g in range(NG):
                    if done is not None and g == 3:
                        b = b_of(done)
                        act.wait_ge(back_mm, b + 2)
                        act.wait_ge(o_mm, b + 1)
                        act.activation(cT[:], k.ps[:, MISC_B, SEQ:2 * SEQ], ACT.Copy).then_inc(back_copied, 1)
                    if old is not None:
                        b = b_of(old)
                        for n, (qt, kt) in enumerate(BLK):
                            act.wait_ge(t_mm, 13 + b * 12 + g * 3 + n + 1)
                            if n == 0:
                                act.wait_ge(pv_mm, b * NG + g + 2)
                            dst = p0[:, g, :, qt * P:qt * P + P] if kt == 0 else p1[:, g, :, :]
                            act.activation(dst, k.ps[:, T_B[(g * 3 + n) % 2], :].rearrange("p (j q) -> p j q", j=4),
                                           ACT.Exp, scale=scale).then_inc(p_ready, 1)

            steps(act, step)

        @block.vector
        def _(dve):
            dve.sem_inc(s_free, 2)
            dve.sem_inc(cx_ready, 2)
            dve.sem_inc(x_added, 1)

            def maxima(batch, g):
                b = b_of(batch)
                if g == 0 and not (isinstance(b, int) and b == 0):
                    dve.wait_ge(neg_ready, b)
                for n, (qt, kt) in enumerate(BLK):
                    dve.wait_ge(s_mm, 13 + b * 12 + g * 3 + n + 1)
                    dve.tensor_reduce(mx[:, n, g * 4:g * 4 + 4],
                                      k.ps[:, S_B[(g * 3 + n) % 2], :].rearrange("p (j q) -> p j q", j=4),
                                      AX.X, ALU.max, negate=True).then_inc(s_free, 1)

            def copy_values(batch, g):
                b = b_of(batch)
                dve.wait_ge(pv_mm, NG + 1 + b * NG + g + 1)
                if g == 0:
                    dve.wait_ge(ct_mm, b * 2 + 1)
                dve.tensor_copy(cx[:, batch[1], g, :], k.ps[:, PV_B[g % 2], 0:SEQ]).then_inc(cx_ready, 1)

            def normalize(batch, qt):
                b = b_of(batch)
                dve.wait_ge(ct_mm, 3 + b * 2 + qt + 1)
                ct = k.ps[:, CT_B, :].rearrange("p (h r) -> p h r", r=32)
                dve.reciprocal(rden[:, qt, :], ct[:, :, HD]).then_inc(den_done, 1)
                dve.wait_ge(den_done, b * 2 + qt + 1)
                if qt == 0:
                    dve.wait_ge(back_mm, b + 1)
                dve.tensor_tensor(cn[:, qt, :].rearrange("p (h d) -> p h d", d=HD), ct[:, :, 0:HD],
                                  rden[:, qt, :].unsqueeze(2).to_broadcast([P, HEADS, HD]),
                                  ALU.mult).then_inc(norm_done, 1)

            def step(new, mid, old, done):
                for g in range(NG):
                    if new is not None:
                        maxima(new, g)
                    if done is not None:
                        if g == 0:
                            copy_values(done, NG - 1)
                        elif g < 3:
                            normalize(done, g - 1)
                    if g == 3 and new is not None:
                        b = b_of(new)
                        dve.wait_ge(s_free, 2 + b * 12 + 12)
                        dve.wait_ge(mt_mm, b + 1)
                        dve.tensor_copy(neg[:, 0, :], mx[:, 0, :])
                        dve.tensor_tensor(neg[:, 1, :], mx[:, 1, :], mx[:, 2, :], ALU.min).then_inc(neg_ready, 1)
                    if old is not None and g > 0:
                        copy_values(old, g - 1)
                if done is not None:
                    b = b_of(done)
                    dve.wait_ge(o_mm, b + 2)
                    xs = k.x[:, sl(b * 2, 2), :]
                    dve.tensor_tensor(xs, xs, k.ps[:, CT_B, 0:SEQ].rearrange("p (t c) -> p t c", c=P),
                                      ALU.add).then_inc(x_added, 1)

            steps(dve, step)



HID1 = 384
KT1 = HID1 // P


def ffn1(k):
    nc, w = k.nc, k.w
    dequant = k.sem("f1_dequant")
    gate_mm, up_mm, sg_ready, h_ready = k.sem("f1_gate"), k.sem("f1_up"), k.sem("f1_silu"), k.sem("f1_h")
    down_mm, added = k.sem("f1_down"), k.sem("f1_add")
    with ExitStack() as st, nc.Block() as block:
        sg = k.sb("f1_sg", [P, KT1, CHUNK], ctx=st)
        h = k.sb("f1_h_sb", [P, 2, KT1, CHUNK], ctx=st)
        wg, wu = k.sb("f1_wg", [P, HID1], ctx=st), k.sb("f1_wu", [P, HID1], ctx=st)
        wd = k.sb("f1_wd", [P, KT1, DM], ctx=st)

        def passes(engine, gated, down):
            gated((0, 0))
            with engine.Fori(0, NCH // 2 - 1) as j:
                gated((j, 1))
                down((j, 0))
                gated((j + 1, 0))
                down((j, 1))
            gated((NCH // 2 - 1, 1))
            down((NCH // 2 - 1, 0))
            down((NCH // 2 - 1, 1))

        @block.gpsimd
        def _(pool):
            for a, b in ((wg, w["f1_gate"]), (wu, w["f1_up"]), (wd, w["f1_down"])):
                pool.tensor_scalar(a[:], b[:], 1.0 / 127.0, None, ALU.mult).then_inc(dequant, 1)

        @block.tensor
        def _(pe):
            pe.wait_ge(dequant, 3)

            def gated(c):
                i = c[0] * 2 + c[1]
                xc = k.xT[:, sl(i * CHUNK, CHUNK)]
                for t in range(KT1):
                    pe.wait_ge(h_ready, i * KT1 + t + 1)
                    pe.matmul(k.ps[:, t, :], wg[:, t * P:t * P + P], xc, start=True, stop=True).then_inc(gate_mm, 1)
                    pe.matmul(k.ps[:, KT1 + t, :], wu[:, t * P:t * P + P], xc, start=True,
                              stop=True).then_inc(up_mm, 1)

            def down(c):
                i = c[0] * 2 + c[1]
                pe.wait_ge(h_ready, KT1 + i * KT1 + KT1)
                pe.wait_ge(added, i + 1)
                for t in range(TPC):
                    for kt in range(KT1):
                        ins = pe.matmul(k.ps[:, 6 + c[1], t * P:t * P + P], h[:, c[1], kt, t * P:t * P + P], wd[:, kt, :],
                                        start=(kt == 0), stop=(kt == KT1 - 1))
                ins.then_inc(down_mm, 1)

            passes(pe, gated, down)

        @block.scalar
        def _(act):
            def gated(c):
                i = c[0] * 2 + c[1]
                for t in range(KT1):
                    act.wait_ge(gate_mm, i * KT1 + t + 1)
                    act.wait_ge(h_ready, i * KT1 + t + 1)
                    act.activation(sg[:, t, :], k.ps[:, t, :], ACT.Silu).then_inc(sg_ready, 1)

            passes(act, gated, lambda c: None)

        @block.vector
        def _(dve):
            dve.sem_inc(h_ready, KT1)
            dve.sem_inc(added, 2)

            def gated(c):
                i = c[0] * 2 + c[1]
                dve.wait_ge(added, i + 1)
                for t in range(KT1):
                    dve.wait_ge(sg_ready, i * KT1 + t + 1)
                    dve.wait_ge(up_mm, i * KT1 + t + 1)
                    dve.tensor_tensor(h[:, c[1], t, :], sg[:, t, :], k.ps[:, KT1 + t, :], ALU.mult).then_inc(h_ready, 1)

            def down(c):
                i = c[0] * 2 + c[1]
                dve.wait_ge(down_mm, i + 1)
                xs = k.x[:, sl(i * TPC, TPC), :]
                dve.tensor_tensor(xs, xs, k.ps[:, 6 + c[1], :].rearrange("p (t c) -> p t c", c=P),
                                  ALU.add).then_inc(added, 1)

            passes(dve, gated, down)



HID2 = 512
KT2 = HID2 // P
WIN = 3


def layer2_body(k):
    nc, w = k.nc, k.w
    prep = k.sem("l2_prep")
    q_mm, copied, pj_ready, s_mm = k.sem("w_qkv"), k.sem("w_copied"), k.sem("w_pj"), k.sem("w_s")
    m_cp, mx_step, d_ready, e_ready = k.sem("w_m"), k.sem("w_mx"), k.sem("w_d"), k.sem("w_e")
    tail_step, y_ready = k.sem("w_tail"), k.sem("w_y")
    a_mm, sg_ready, h_ready = k.sem("f2_a"), k.sem("f2_sg"), k.sem("f2_h")
    b_mm, g1_done, c_mm, g2_done = k.sem("f2_b"), k.sem("f2_g1"), k.sem("f2_c"), k.sem("f2_g2")
    d_mm, x_added = k.sem("f2_d"), k.sem("f2_x")
    OUT_B, W_B = 4, (5, 6, 7)
    scale = 1.0 / float(HD) ** 0.5
    MXS, TLS = 2, 10
    with ExitStack() as st, nc.Block() as block:
        h1 = k.sb("f2_h1", [P, KT2, CHUNK], ctx=st)
        h2 = k.sb("f2_h2", [P, KT2, CHUNK], ctx=st)
        h3 = k.sb("f2_h3", [P, KT2, CHUNK], ctx=st)
        sg = k.sb("f2_sg_sb", [P, 2, CHUNK], ctx=st)
        q = k.sb("w_q_sb", [P, 2, SEQ], ctx=st)
        kk = k.sb("w_k_sb", [P, 2, WIN - 1 + SEQ], ctx=st)
        v = k.sb("w_v_sb", [P, 2, WIN - 1 + SEQ], ctx=st)
        pj = k.sb("w_pj_sb", [P, WIN, 2, SEQ], ctx=st)
        mx = k.sb("w_mx_sb", [P, 2, SEQ], ctx=st)
        e = k.sb("w_e_sb", [P, WIN, 2, SEQ], ctx=st)
        den = k.sb("w_den", [P, 2, SEQ], ctx=st)
        rden = k.sb("w_rden", [P, 2, SEQ], ctx=st)
        y = k.sb("w_y_sb", [P, CHUNK], ctx=st)
        xh, xl = k.sb("f2_x_hi", [P, BATCH * SEQ], F16, ctx=st), k.sb("f2_x_lo", [P, BATCH * SEQ], F16, ctx=st)
        hi_done, lo_done = k.sem("f2_xh"), k.sem("f2_xl")

        def bank(n):
            return k.ps[:, n, :].rearrange("p (b t) -> p b t", b=2)

        def shifted(a, j):
            return a[:, :, WIN - 1 - j:WIN - 1 - j + SEQ]

        @block.gpsimd
        def _(pool):
            pool.memset(kk[:], 0.0).then_inc(prep, 1)
            pool.memset(v[:], 0.0).then_inc(prep, 1)
            pool.tensor_tensor(w["w3"][:], w["w3"][:], w["s3"][:].unsqueeze(1).to_broadcast([P, KT2, DM]),
                               ALU.mult).then_inc(prep, 1)
            pool.tensor_tensor(k.x[:], k.x[:], w["a2bo"][:].unsqueeze(1).to_broadcast([P, TILES, DM]),
                               ALU.add).then_inc(prep, 1)

            with pool.Fori(0, NCH) as i:
                at = sl(i * CHUNK, CHUNK)
                pool.tensor_copy(xh[:, at], k.xT[:, at]).then_inc(hi_done, 1)
                pool.wait_ge(hi_done, i + 1)
                pool.tensor_tensor(xl[:, at], k.xT[:, at], xh[:, at], ALU.subtract).then_inc(lo_done, 1)

        @block.tensor
        def _(pe):
            pe.sem_inc(s_mm, 3)
            pe.sem_inc(b_mm, 4)
            pe.sem_inc(c_mm, 4)
            pe.sem_inc(d_mm, 1)
            pe.wait_ge(prep, 4)
            with pe.Fori(0, NCH // 2) as pair:
                for i in (pair * 2, pair * 2 + 1):
                    at = sl(i * CHUNK, CHUNK)

                    def product(bank, name, t):
                        hi, lo = (part[name][:, t * P:t * P + P] for part in (k.w_hi, k.w_lo))
                        pe.matmul(k.ps[:, bank, :], hi, xh[:, at], start=True, stop=False)
                        pe.matmul(k.ps[:, bank, :], hi, xl[:, at], start=False, stop=False)
                        return pe.matmul(k.ps[:, bank, :], lo, xh[:, at], start=False, stop=True)

                    pe.wait_ge(hi_done, i + 1)
                    pe.wait_ge(lo_done, i + 1)
                    pe.wait_ge(d_ready, i + 1)
                    for n, name in enumerate(("a2q", "a2k", "a2v")):
                        product(W_B[n], name, 0).then_inc(q_mm, 1)
                    for t in range(KT2):
                        if t == 0:
                            pe.wait_ge(g2_done, i * 4 + 4)
                        if t > 1:
                            pe.wait_ge(h_ready, 2 + i * 4 + t - 1)
                        product(t % 2, "w1", t).then_inc(a_mm, 1)
                        product(2 + t % 2, "w2", t).then_inc(a_mm, 1)
                    for j in range(WIN):
                        pe.wait_ge(copied, i * 3 + 3)
                        pe.wait_ge(pj_ready, 3 + i * 3 + j + 1)
                        pe.matmul(k.ps[:, W_B[j], :], w["heads"][:], pj[:, j].rearrange("p b t -> p (b t)"),
                                  start=True, stop=True).then_inc(s_mm, 1)
                    for t in range(KT2):
                        for kt in range(KT2):
                            if t == 0:
                                pe.wait_ge(h_ready, 2 + i * 4 + max(3, kt + 1))
                            ins = pe.matmul(k.ps[:, t, :], w["h1"][:, kt, t * P:t * P + P], h1[:, kt, :],
                                            start=(kt == 0), stop=(kt == KT2 - 1))
                        ins.then_inc(b_mm, 1)
                    for t in range(KT2):
                        for kt in range(KT2):
                            if t == 0 or kt == 0:
                                pe.wait_ge(g1_done, i * 4 + max(t, kt) + 1)
                            ins = pe.matmul(k.ps[:, t, :], w["h2"][:, kt, t * P:t * P + P], h2[:, kt, :],
                                            start=(kt == 0), stop=(kt == KT2 - 1))
                        ins.then_inc(c_mm, 1)
                    pe.wait_ge(x_added, i + 1)
                    for kt in range(KT2):
                        pe.wait_ge(g2_done, 4 + i * 4 + kt + 1)
                        for t in range(TPC):
                            pe.matmul(k.ps[:, OUT_B, t * P:t * P + P], h3[:, kt, t * P:t * P + P], w["w3"][:, kt, :],
                                      start=(kt == 0 and t == 0), stop=False, skip_group_check=True)
                    pe.wait_ge(y_ready, 1 + i + 1)
                    for t in range(TPC):
                        ins = pe.matmul(k.ps[:, OUT_B, t * P:t * P + P], y[:, t * P:t * P + P], w["a2o"][:],
                                        start=False, stop=True, skip_group_check=True)
                    ins.then_inc(d_mm, 1)

        @block.scalar
        def _(act):
            act.sem_inc(g2_done, 4)
            act.wait_ge(prep, 2)
            with act.Fori(0, NCH // 2) as pair:
                for i in (pair * 2, pair * 2 + 1):
                    for n, (dst, b) in enumerate(((q[:], "a2bq"), (kk[:, :, 2:], "a2bk"), (v[:, :, 2:], "a2bv"))):
                        act.wait_ge(q_mm, i * 3 + n + 1)
                        if n == 0:
                            act.wait_ge(pj_ready, i * 3 + 3)
                        if n == 2:
                            act.wait_ge(y_ready, i + 1)
                        act.activation(dst, bank(W_B[n]), ACT.Identity, bias=w[b][:, 0:1]).then_inc(copied, 1)
                    for t in range(KT2):
                        act.wait_ge(a_mm, i * 8 + 2 * t + 1)
                        act.wait_ge(h_ready, i * 4 + t + 1)
                        act.activation(sg[:, t % 2, :], k.ps[:, t % 2, :], ACT.Silu,
                                       scale=w["s1"][:, t:t + 1]).then_inc(sg_ready, 1)
                    act.wait_ge(s_mm, 3 + i * 3 + 1)
                    act.wait_ge(d_ready, i + 1)
                    act.activation(mx[:], bank(W_B[0]), ACT.Copy).then_inc(m_cp, 1)
                    act.wait_ge(d_ready, 1 + i + 1)
                    act.activation(e[:], e[:], ACT.Exp, scale=scale).then_inc(e_ready, 1)
                    for t in range(KT2):
                        act.wait_ge(b_mm, 4 + i * 4 + t + 1)
                        act.wait_ge(c_mm, i * 4 + 4)
                        act.activation(h2[:, t, :], k.ps[:, t, :], ACT.Gelu, scale=w["hs1"][:, t:t + 1]).then_inc(g1_done, 1)
                    for t in range(KT2):
                        act.wait_ge(c_mm, 4 + i * 4 + t + 1)
                        act.wait_ge(d_mm, i + 1)
                        act.activation(h3[:, t, :], k.ps[:, t, :], ACT.Gelu, scale=w["hs2"][:, t:t + 1]).then_inc(g2_done, 1)

        @block.vector
        def _(dve):
            dve.sem_inc(pj_ready, 3)
            dve.sem_inc(h_ready, 2)
            dve.sem_inc(d_ready, 1)
            dve.sem_inc(y_ready, 1)
            dve.sem_inc(x_added, 1)
            dve.wait_ge(prep, 4)
            with dve.Fori(0, NCH // 2) as pair:
                for i in (pair * 2, pair * 2 + 1):
                    n = 0

                    def link(ins):
                        nonlocal n
                        n += 1
                        ins.then_inc(tail_step, 1)
                        dve.wait_ge(tail_step, i * TLS + n)

                    dve.wait_ge(copied, i * 3 + 2)
                    dve.wait_ge(s_mm, i * 3 + 3)
                    for j in range(WIN):
                        dve.tensor_tensor(pj[:, j], q[:], shifted(kk, j), ALU.mult).then_inc(pj_ready, 1)
                    dve.wait_ge(b_mm, i * 4 + 4)
                    for t in range(KT2):
                        dve.wait_ge(sg_ready, i * 4 + t + 1)
                        dve.wait_ge(a_mm, i * 8 + 2 * t + 2)
                        dve.scalar_tensor_tensor(out=h1[:, t, :], in0=k.ps[:, 2 + t % 2, :], scalar=w["s2"][:, t:t + 1],
                                                 in1=sg[:, t % 2, :], op0=ALU.mult, op1=ALU.mult).then_inc(h_ready, 1)
                    dve.wait_ge(m_cp, i + 1)
                    dve.wait_ge(s_mm, 3 + i * 3 + 3)
                    for j in (1, 2):
                        dve.tensor_tensor(mx[:, :, j:], mx[:, :, j:], bank(W_B[j])[:, :, j:], ALU.max).then_inc(mx_step, 1)
                        dve.wait_ge(mx_step, i * MXS + j)
                    for j in range(WIN):
                        ins = dve.tensor_tensor(e[:, j], bank(W_B[j]), mx[:], ALU.subtract)
                    ins.then_inc(d_ready, 1)
                    dve.wait_ge(e_ready, i + 1)
                    dve.memset(e[:, 1, :, 0:1], 0.0)
                    link(dve.memset(e[:, 2, :, 0:2], 0.0))
                    link(dve.tensor_tensor(den[:], e[:, 0], e[:, 1], ALU.add))
                    link(dve.tensor_tensor(den[:], den[:], e[:, 2], ALU.add))
                    link(dve.reciprocal(rden[:], den[:]))
                    for j in range(WIN):
                        link(dve.tensor_tensor(e[:, j], e[:, j], shifted(v, j), ALU.mult))
                    link(dve.tensor_tensor(e[:, 0], e[:, 0], e[:, 1], ALU.add))
                    link(dve.tensor_tensor(e[:, 0], e[:, 0], e[:, 2], ALU.add))
                    dve.wait_ge(d_mm, i + 1)
                    link(dve.tensor_tensor(den[:], e[:, 0], rden[:], ALU.mult))
                    dve.tensor_copy(y[:].rearrange("p (b t) -> p b t", b=2), den[:]).then_inc(y_ready, 1)
                    assert n == TLS
                    dve.wait_ge(d_mm, 1 + i + 1)
                    xs = k.x[:, sl(i * TPC, TPC), :]
                    dve.tensor_tensor(xs, xs, k.ps[:, OUT_B, :].rearrange("p (t c) -> p t c", c=P),
                                      ALU.add).then_inc(x_added, 1)


def layer2_weights(k, c, weight, everywhere, column):
    d = k.dram
    for n in "qkvo":
        weight(c, "a2" + n, [P, DM], d[f"a2{n}T"])
    for n in "qkv":
        column(c, "a2b" + n, d["L2_attn_b" + n])
    everywhere(c, "a2bo", d["L2_attn_bo"])
    everywhere(c, "s3", d["L2_ffn_w3_s"])
    weight(c, "heads", [P, P], d["head_blocks"])
    for n in ("w1", "w2"):
        weight(c, n, [P, HID2], d[f"f2_{n}T"])
    for n, s in (("s1", "w1_s"), ("s2", "w2_s"), ("hs1", "h1_s"), ("hs2", "h2_s")):
        weight(c, n, [P, KT2], d[f"f2_{s}"])
    for n in ("h1", "h2"):
        weight(c, n, [P, KT2, HID2], d[f"f2_{n}T"].rearrange("(t p) o -> p t o", p=P))
    weight(c, "w3", [P, KT2, DM], d["f2_w3T"].rearrange("(t p) o -> p t o", p=P))


L2_SPLIT = ("a2q", "a2k", "a2v", "w1", "w2")


def layer2(k):
    loads_arrived(k, 2)
    with ExitStack() as c:
        for part, name in ((k.w_hi, "hi"), (k.w_lo, "lo")):
            for n in L2_SPLIT:
                part[n] = k.sb(f"w_{name}_{n}", list(k.w[n].shape), F16, ctx=c)
        norm(k, "n2", k.x, k.xT, split=L2_SPLIT)
        layer2_body(k)



CYCLES = 3


def global_net(k, beta):
    nc, w = k.nc, k.w
    v, a, m = k.sem("g_dve"), k.sem("g_act"), k.sem("g_pe")
    with ExitStack() as st, nc.Block() as block:
        mean = k.sb("g_mean", [P, BATCH], ctx=st)
        g1, g2 = k.sb("g_h1", [P, BATCH], ctx=st), k.sb("g_h2", [P, BATCH], ctx=st)
        t3 = k.sb("g_t", [P, BATCH], ctx=st)

        @block.vector
        def _(dve):
            dve.tensor_reduce(mean[:], k.xT[:].rearrange("p (b t) -> p b t", b=BATCH), AX.X, ALU.add).then_inc(v, 1)
            dve.wait_ge(v, 1)
            dve.tensor_scalar(mean[:], mean[:], 1.0 / SEQ, None, ALU.mult).then_inc(v, 1)
            dve.tensor_scalar(k.alpha[:], w["ar"][:], 0.3, None, ALU.mult).then_inc(v, 1)
            dve.tensor_scalar(k.hb4[:], w["cb4"][:], 0.5, None, ALU.mult).then_inc(v, 1)
            dve.tensor_scalar(k.hgb[:], w["gb3"][:], 0.5, None, ALU.mult).then_inc(v, 1)
            dve.wait_ge(a, 3)
            dve.tensor_scalar(beta[:], t3[:], 0.7, None, ALU.mult).then_inc(v, 1)
            dve.wait_ge(v, 6)
            dve.tensor_scalar(beta[:], beta[:], w["ar"][:, 0:1], 0.1, ALU.mult, ALU.add).then_inc(v, 1)

        @block.tensor
        def _(pe):
            pe.wait_ge(v, 2)
            pe.matmul(k.ps[:, 0, 0:BATCH], w["gw1"][:], mean[:], start=True, stop=True).then_inc(m, 1)
            pe.wait_ge(a, 1)
            pe.matmul(k.ps[:, 1, 0:BATCH], w["gw2"][:], g1[:], start=True, stop=True).then_inc(m, 1)
            pe.wait_ge(a, 2)
            pe.matmul(k.ps[:, 2, 0:BATCH], w["gw3"][:], g2[:], start=True, stop=True).then_inc(m, 1)

        @block.scalar
        def _(act):
            act.wait_ge(m, 1)
            act.activation(g1[:], k.ps[:, 0, 0:BATCH], ACT.Gelu, bias=w["gb1"][:, 0:1]).then_inc(a, 1)
            act.wait_ge(m, 2)
            act.activation(g2[:], k.ps[:, 1, 0:BATCH], ACT.Gelu, bias=w["gb2"][:, 0:1]).then_inc(a, 1)
            act.wait_ge(m, 3)
            act.wait_ge(v, 5)
            act.activation(t3[:], k.ps[:, 2, 0:BATCH], ACT.Tanh, bias=k.hgb[:, 0:1], scale=0.5).then_inc(a, 1)


def coupling(k, beta):
    nc, w = k.nc, k.w
    mm = [k.sem(f"c_mm{c}") for c in range(2)]
    fn = [k.sem(f"c_fn{c}") for c in range(2)]
    dv = [k.sem(f"c_dv{c}") for c in range(2)]
    MM, FN, DV = CYCLES * 5 + 1, CYCLES * 4, CYCLES * 4 + 1
    with ExitStack() as st, nc.Block() as block:
        g = [k.sb(f"c_g{c}", [P, 3, CHUNK], ctx=st) for c in range(2)]
        tn = [k.sb(f"c_tanh{c}", [P, 2, SEQ], ctx=st) for c in range(2)]
        tw = [k.sb(f"c_tw{c}", [P, CHUNK], ctx=st) for c in range(2)]
        fin = [k.sb(f"c_fin{c}", [P, CHUNK], ctx=st) for c in range(2)]

        def chunk(i, c):
            return k.xT[:, sl(i * 2 * CHUNK + c * CHUNK, CHUNK)]

        @block.tensor
        def _(pe):
            with pe.Fori(0, NCH // 2) as i:
                for y in range(CYCLES):
                    for layer in range(4):
                        for c in range(2):
                            if layer == 0:
                                pe.wait_ge(dv[c], DV + i * DV + y * 4)
                                pe.matmul(k.ps[:, 4 * c + 3, :], w["twist"][:], chunk(i, c), start=True,
                                          stop=True).then_inc(mm[c], 1)
                                src = chunk(i, c)
                            else:
                                pe.wait_ge(fn[c], i * FN + y * 4 + layer)
                                src = g[c][:, layer - 1, :]
                            pe.matmul(k.ps[:, 4 * c + layer % 3, :], w[f"cw{layer + 1}"][:], src, start=True,
                                      stop=True).then_inc(mm[c], 1)
                for c in range(2):
                    pe.wait_ge(dv[c], DV + i * DV + CYCLES * 4)
                    for t in range(TPC):
                        ins = pe.transpose(k.ps[:, 4 * c + 3, t * P:t * P + P], fin[c][:, t * P:t * P + P], k.ident[:])
                    ins.then_inc(mm[c], 1)

        @block.scalar
        def _(act):
            with act.Fori(0, NCH // 2) as i:
                for y in range(CYCLES):
                    for layer in range(3):
                        for c in range(2):
                            act.wait_ge(mm[c], i * MM + y * 5 + layer + 2)
                            act.activation(g[c][:, layer, :], k.ps[:, 4 * c + layer, :], ACT.Gelu,
                                           bias=w[f"cb{layer + 1}"][:, 0:1]).then_inc(fn[c], 1)
                    for c in range(2):
                        act.wait_ge(mm[c], i * MM + y * 5 + 5)
                        act.wait_ge(dv[c], DV + i * DV + y * 4)
                        act.activation(tn[c][:].rearrange("p b t -> p (b t)"), k.ps[:, 4 * c, :], ACT.Tanh,
                                       bias=k.hb4[:, 0:1], scale=0.5).then_inc(fn[c], 1)

        @block.vector
        def _(dve):
            for c in range(2):
                dve.sem_inc(dv[c], DV)
            with dve.Fori(0, NCH // 2) as i:
                for y in range(CYCLES):
                    for c in range(2):
                        at = i * DV + y * 4 + DV
                        dve.wait_ge(fn[c], i * FN + y * 4 + 4)
                        for b in range(2):
                            dve.tensor_scalar(tn[c][:, b, :], tn[c][:, b, :], k.alpha[:, 0:1],
                                              beta[:, sl(i * 4 + c * 2 + b, 1)], ALU.mult, ALU.add).then_inc(dv[c], 1)
                        dve.wait_ge(dv[c], at + 2)
                        dve.tensor_tensor(tw[c][:], tn[c][:].rearrange("p b t -> p (b t)"), k.ps[:, 4 * c + 3, :],
                                          ALU.mult).then_inc(dv[c], 1)
                        dve.wait_ge(dv[c], at + 3)
                        dst = chunk(i, c) if y < CYCLES - 1 else fin[c][:]
                        dve.tensor_tensor(dst, chunk(i, c), tw[c][:], ALU.add).then_inc(dv[c], 1)
                for c in range(2):
                    dve.wait_ge(mm[c], i * MM + MM)
                    xs = k.x[:, sl(i * 2 * TPC + c * TPC, TPC), :]
                    dve.tensor_tensor(xs, xs, k.ps[:, 4 * c + 3, :].rearrange("p (t c) -> p t c", c=P),
                                      ALU.add).then_inc(dv[c], 1)


def layer3_weights(k, c, weight, column):
    d = k.dram
    for n in "qkvo":
        weight(c, "a3" + n, [P, DM], d[f"a3{n}T"])
    for n in ("cw1", "cw2", "cw3", "cw4", "gw1", "gw2", "gw3"):
        weight(c, n, [P, P], d[n])
    weight(c, "twist", [P, P], d["twist"])
    for n in ("cb1", "cb2", "cb3", "cb4", "gb1", "gb2", "gb3", "ar"):
        column(c, n, d[n])
    k.alpha, k.hb4, k.hgb = k.sb("alpha", [P, 1], ctx=c), k.sb("half_b4", [P, 1], ctx=c), k.sb("half_gb", [P, 1], ctx=c)
    k.beta = k.sb("beta_b", [P, BATCH], ctx=c)


def layer3(k):
    w, beta = k.w, k.beta
    loads_arrived(k, 3)
    norm(k, "n3", k.x, k.xT)
    with ExitStack() as a:
        k.v = k.sb("v_all3", [P, TILES, DM], ctx=a)
        project(k, "pr3", k.xT, w["a3q"], w["a3k"], w["a3v"], None)
        attend(k, "at3", w["a3o"])
    global_net(k, beta)
    coupling(k, beta)


def store(k):
    done = k.sem("out_stored")
    with k.nc.Block() as block:

        @block.sync
        def _(sp):
            sp.dma_start(k.out.rearrange("b (h p) d -> p (b h) d", p=P), k.x[:]).then_inc(done, 16)
            sp.wait_ge(done, 16)


UPTO = 99


def loads_arrived(k, layer):
    arrived, loads = k.late[layer]
    with k.nc.Block() as block:

        @block.sync
        def _(sp):
            sp.wait_ge(arrived, 16 * len(loads))


def layer1_weights(k, c, weight, everywhere):
    d = k.dram
    for n in "qkvo":
        weight(c, "a1" + n, [P, DM], d["L1_attn_W" + n])
    everywhere(c, "a1bo", d["L1_attn_bo"])
    weight(c, "f1_gate", [P, HID1], d["f1_gateT"], I32)
    weight(c, "f1_up", [P, HID1], d["f1_upT"], I32)
    weight(c, "f1_down", [P, KT1, DM], d["f1_downT"].rearrange("(t p) c -> p t c", p=P), I32)


def layer1(k):
    loads_arrived(k, 1)
    norm(k, "n1", k.x, k.xT)
    w = k.w
    with ExitStack() as a:
        k.v = k.sb("v_all1", [P, TILES, DM], ctx=a)
        project(k, "pr1", k.xT, w["a1q"], w["a1k"], w["a1v"], w["a1bo"])
        attend(k, "at1", w["a1o"])
    ffn1(k)


def build(nc, dram, out):
    with ExitStack() as ctx:
        k = Program(nc, ctx, dram, out)
        k.ps = ctx.enter_context(nc.psum_tensor("banks", [P, 8, 512], F32))
        k.x = k.sb("x_res", [P, TILES, DM])
        k.xT = k.sb("xnT", [P, BATCH * SEQ])
        k.ident, k.ident16 = k.sb("ident", [P, P]), k.sb("ident16", [P, P], F16)
        k.mirror = k.sb("mirror", [P, P])
        k.mask_kq, k.mask_qk = k.sb("mask_kq", [P, 4, P], F16), k.sb("mask_qk", [P, 4, P], F16)
        k.eps = k.sb("eps", [P, 1])
        k.lag_i, k.lag = k.sb("lag_i", [P, SEQ], I32), k.sb("lag", [P, SEQ])
        k.st, k.mv = k.sb("ln_stats", [P, TILES, 6]), k.sb("ln_mv", [P, TILES, 2])
        k.std, k.rstd, k.z8 = k.sb("ln_std", [P, TILES]), k.sb("ln_rstd", [P, TILES]), k.sb("ln_z", [P, 8, DM])
        k.kpad = nc.dram_tensor("kernel_padded", (DM, P + SEQ), F32).ap()
        k.yT = nc.dram_tensor("conv_out", (DM, BATCH, SEQ), F32).ap()
        k.qs = nc.dram_tensor("q_stacked", (BATCH, P, ROWS, SEQ), F16).ap()
        k.ks = nc.dram_tensor("k_stacked", (BATCH, P, ROWS, SEQ), F16).ap()
        k.w, k.loads = {}, []

        def weight(c, name, shape, src, dt=F32):
            k.w[name] = k.sb("w_" + name, shape, dt, ctx=c)
            k.loads.append((k.w[name][:], src))

        def column(c, name, src):
            weight(c, name, [P, 1], src.rearrange("(p a) -> p a", a=1))

        def everywhere(c, name, src):
            weight(c, name, [P, DM], bass.AP(tensor=src.tensor, offset=src.offset, ap=[[0, P], [1, DM]]))

        k.late = {}
        for layer, declare in ((1, lambda: layer1_weights(k, ctx, weight, everywhere)),
                               (2, lambda: layer2_weights(k, ctx, weight, everywhere, column)),
                               (3, lambda: layer3_weights(k, ctx, weight, column))):
            declare()
            k.late[layer] = (ctx.enter_context(nc.semaphore(f"weights{layer}_arrived")), k.loads)
            k.loads = []
        with ExitStack() as l0:
            column(l0, "ffn_scale", dram["L0_ffn_ln_scale"])
            column(l0, "ffn_bias", dram["L0_ffn_ln_bias"])
            column(l0, "log_dt", dram["L0_attn_log_dt"])
            column(l0, "D", dram["L0_attn_D_param"])
            everywhere(l0, "gamma", dram["L0_attn_ln_gamma"])
            everywhere(l0, "beta", dram["L0_attn_ln_beta"])
            everywhere(l0, "b_out", dram["L0_attn_b_out"])
            weight(l0, "log_A", [P, NST], dram["L0_attn_log_A"])
            weight(l0, "B", [P, NST], dram["L0_attn_B_param"])
            weight(l0, "C", [P, NST], dram["L0_attn_C_param"])
            weight(l0, "gate", [P, NE], dram["gate_wT"])
            weight(l0, "W_out", [P, DM], dram["W_outT"])
            for n in "gu":
                k.w["W" + n] = k.sb("w_W" + n, [P, NE + 1, INTER], ctx=l0)
                k.loads.append((k.w["W" + n][:, 0:NE, :], dram["L0_ffn_W" + n].rearrange("e p i -> p e i")))
                k.loads.append((k.w["W" + n][:, NE, :], dram["L0_ffn_sW" + n]))
            k.w["Wd"] = k.sb("w_Wd", [P, NE + 1, IT, DM], ctx=l0)
            for e in range(NE):
                k.loads.append((k.w["Wd"][:, e], dram["L0_ffn_Wd"][e].rearrange("(t p) d -> p t d", p=P)))
            k.loads.append((k.w["Wd"][:, NE], dram["L0_ffn_sWd"].rearrange("(t p) d -> p t d", p=P)))
            k.w_hi = {n: k.sb(f"w_hi_{n}", [P, NE + 1, INTER], F16, ctx=l0) for n in "gu"}
            k.w_lo = {n: k.sb(f"w_lo_{n}", [P, NE + 1, INTER], F16, ctx=l0) for n in "gu"}
            gate_weight = k.sb("gate_weight", [P, TILES, NE], ctx=l0)
            k.late[0] = (ctx.enter_context(nc.semaphore("weights0_arrived")), k.loads)
            k.loads = []
            load(k)
            with ExitStack() as mid:
                u = k.sb("ssm_in", [P, 2, DM, BATCH], ctx=mid)
                with ExitStack() as early:
                    z1 = k.sb("xn_tok", [P, TILES, DM], ctx=early)
                    s2 = k.sb("second_rstd", [P, TILES], ctx=early)
                    norm(k, "n0", k.x, k.xT, z1, [late for layer, late in k.late.items() if 0 < layer < UPTO])
                    loads_arrived(k, 0)
                    gates(k, z1, s2, gate_weight)
                    ssm_kernel(k, z1, s2, u)
                convolve(k, u)
            experts(k, k.xT, gate_weight)
        k.end_layer()
        if UPTO >= 2:
            layer1(k)
            k.end_layer()
        if UPTO >= 3:
            layer2(k)
            k.end_layer()
        if UPTO >= 4:
            layer3(k)
        store(k)


_OUTS = [((BATCH, SEQ, DM), "float32")]


TRANSPOSED = {"gate_wT": "L0_ffn_gate_w", "W_outT": "L0_attn_W_out", "f1_gateT": "L1_ffn_w_gate",
              "f1_upT": "L1_ffn_w_up", "f1_downT": "L1_ffn_w_down", "f2_w1T": "L2_ffn_w1_w",
              "f2_w2T": "L2_ffn_w2_w", "f2_h1T": "L2_ffn_h1_w", "f2_h2T": "L2_ffn_h2_w", "f2_w3T": "L2_ffn_w3_w"}
TRANSPOSED |= {f"a{layer}{n}T": f"L{layer}_attn_W{n}" for layer in (2, 3) for n in "qkvo"}


def kernel(**inputs):
    import numpy as np
    import concourse.bacc as bacc
    from concourse.bass_utils import run_bass_kernel_spmd

    nc = bacc.Bacc("TRN2", target_bir_lowering=False, num_devices=1)
    arrays = {n: np.ascontiguousarray(a) for n, a in inputs.items()}
    for new, old in TRANSPOSED.items():
        arrays[new] = np.ascontiguousarray(arrays.pop(old).T)
    for s in ("w1_s", "w2_s", "h1_s", "h2_s"):
        arrays[f"f2_{s}"] = np.ascontiguousarray(arrays.pop(f"L2_ffn_{s}").reshape(-1, P).T)
    for net, n_layers in (("c", 4), ("g", 3)):
        for n in range(1, n_layers + 1):
            a, b = arrays.pop(f"L3_ffn_{net}{'nc'[net == 'g']}_w{n}"), arrays.pop(f"L3_ffn_{net}{'nc'[net == 'g']}_b{n}")
            if n == n_layers:
                a, b = np.repeat(a, P, axis=1), np.repeat(b, P)
            arrays[f"{net}w{n}"] = np.pad(a, ((0, P - a.shape[0]), (0, P - a.shape[1])))
            arrays[f"{net}b{n}"] = np.pad(b, (0, P - b.shape[0]))
    arrays["ar"] = np.repeat(arrays.pop("L3_ffn_adaptive_range"), P)
    arrays["head_blocks"] = np.kron(np.eye(HEADS), np.ones((HD, HD))).astype(np.float32)
    twist, q = np.zeros((P, P), np.float32), np.eye(P // 4, dtype=np.float32)
    for dst, (src, sign) in enumerate(((2, 1), (3, -1), (0, -1), (1, 1))):
        twist[src * 32:src * 32 + 32, dst * 32:dst * 32 + 32] = sign * q
    arrays["twist"] = twist
    dram = {n: nc.dram_tensor(n, a.shape, mybir.dt.from_np(a.dtype), kind="ExternalInput").ap()
            for n, a in arrays.items()}
    shape, dtype = _OUTS[0]
    out = nc.dram_tensor("out", shape, mybir.dt.from_np(np.dtype(dtype)), kind="ExternalOutput").ap()
    build(nc, dram, out)
    r = run_bass_kernel_spmd(nc, [arrays], core_ids=[0])
    return r.results[0]["out"]
```
